# Optimizing a Trainium2 kernel written in Bass

```python
import numpy as np
import jax
import jax.numpy as jnp

def _softmax(x, axis=-1):
    return jax.nn.softmax(x, axis=axis)

def _gelu(x):
    return jax.nn.gelu(x, approximate=True)

def _silu(x):
    return jax.nn.silu(x)

def _sigmoid(x):
    return jax.nn.sigmoid(x)

def _layernorm(x, axis=-1, eps=1e-05):
    m = jnp.mean(x, axis=axis, keepdims=True)
    v = jnp.var(x, axis=axis, keepdims=True)
    return (x - m) / jnp.sqrt(v + eps)

def _scatter_add(tgt, idx, src, axis=0):
    return tgt.at[idx].add(src)

def _segment_sum(src, seg, n):
    return jax.ops.segment_sum(src, seg, n)
kernel_name = 'mk_adj_resnorm_d1_adj_r2_bf0363'

def setup_inputs(seed: int=0):
    np.random.seed(seed)
    _w = jnp.asarray

    def _rec_inputs():
        import jax
        import jax.numpy as jnp
        _gk = jax.random.key(seed)
        x = -0.000929 + 1 * jax.random.normal(jax.random.fold_in(_gk, 1), (8192, 128), jnp.float32)
        _a = jax.random.bernoulli(jax.random.fold_in(_gk, 2), 0.000244141, (8192, 8192))
        adj = _a.astype(jnp.int32)
        return (x, adj)
    x, adj = _rec_inputs()

    def _L0_gnn_setup():
        import jax, jax.numpy as jnp
        import numpy as np
        N = 4096
        D_IN = 128
        D_OUT = 128
        ALPHA = 0.2
        NEG = -9000000000000000.0
        key = jax.random.key(seed)
        k1, k2, k3, k4 = jax.random.split(key, 4)
        input = jax.random.normal(k1, (N, D_IN), dtype=jnp.float32)
        adj = jax.random.randint(k2, (N, N), 0, 2, dtype=jnp.int32)
        lim_w = 1.414 * np.sqrt(6.0 / (D_IN + D_OUT))
        W = jax.random.uniform(k3, (D_IN, D_OUT), jnp.float32, -lim_w, lim_w)
        lim_a = 1.414 * np.sqrt(6.0 / (2 * D_OUT + 1))
        a = jax.random.uniform(k4, (2 * D_OUT, 1), jnp.float32, -lim_a, lim_a)
        return {'input': input, 'adj': adj, 'W': W, 'a': a}
    _L0_gnn_all = _L0_gnn_setup()
    _L0_gnn_in = {k: v for k, v in _L0_gnn_all.items() if k in ('W', 'a')}
    del _L0_gnn_all
    return {'x': x, 'adj': adj, 'L0_gnn_W': _L0_gnn_in['W'], 'L0_gnn_a': _L0_gnn_in['a']}

def reference(x, adj, L0_gnn_W, L0_gnn_a):
    import jax
    import jax.numpy as jnp

    def _L0_gnn_ref(input, adj, W, a):
        import jax, jax.numpy as jnp
        import numpy as np
        N = 4096
        D_IN = 128
        D_OUT = 128
        ALPHA = 0.2
        NEG = -9000000000000000.0
        h = input @ W
        a1 = a[:D_OUT, 0]
        a2 = a[D_OUT:, 0]
        e = (h @ a1)[:, None] + (h @ a2)[None, :]
        e = jnp.where(e > 0, e, ALPHA * e)
        e = jnp.where(adj > 0, e, NEG)
        attention = jax.nn.softmax(e, axis=1)
        h_prime = attention @ h
        return jax.nn.elu(h_prime)
    x = _layernorm(x + _L0_gnn_ref(x, adj, L0_gnn_W, L0_gnn_a), axis=-1)
    return x

_drawn_inputs = setup_inputs


def setup_inputs(seed=0):
    import zlib

    import numpy as np

    out = dict(_drawn_inputs(seed))
    spreads = {}
    factors = {}
    for name, (base, spread) in spreads.items():
        noise = np.random.default_rng([zlib.crc32(name.encode()), seed]).standard_normal(out[name].shape)
        drawn = base * np.exp(spread * noise) if base else spread * noise
        out[name] = jnp.asarray(drawn.astype(out[name].dtype))
    for name, factor in factors.items():
        out[name] = (out[name] * factor).astype(out[name].dtype)
    return out
```

```python
from contextlib import ExitStack

import concourse.bass as bass
from concourse import mybir

SLOTS = 10
NEG = -9000000000000000.0
ALPHA = 0.2
EPS = 1e-5


class Steps:

    def __init__(self, eng, sem):
        self.eng, self.sem, self.n = eng, sem, 0

    def after(self, instruction):
        self.n += 1
        instruction.then_inc(self.sem, 1)
        self.eng.wait_ge(self.sem, self.n)


def hold(eng, sem, value, spare):
    eng.wait_ge(sem, value)
    eng.sem_inc(spare, 1)


def graph_attention(nc, x, adj, W, a, out):
    fp32, i32, u32, bf16 = mybir.dt.float32, mybir.dt.int32, mybir.dt.uint32, mybir.dt.bfloat16
    ACT, ALU, AX = mybir.ActivationFunctionType, mybir.AluOpType, mybir.AxisListType

    N, D = x.shape
    P = 128
    assert D == P and adj.shape[0] == N and adj.shape[1] == N
    TILES = N // P
    ROW = D + 2
    T_COL, S_COL = D, D + 1
    HALF = N // 2
    BITS = 8
    FOLD = HALF // BITS
    assert FOLD == 512
    PAIR = 2
    GROUPS = 2
    BODY = PAIR * GROUPS
    BODIES = TILES // BODY
    HALVES = 2 * BODY
    LOAD_SLOTS = 4
    CAND = 2 * 8 * BITS
    PRO = 4
    PRO_STEPS = TILES // PRO

    adj_tiles = adj.rearrange("(t p) c -> t p c", p=P)
    out_tiles = out.rearrange("(t p) c -> p t c", p=P)
    x_tiles = x.rearrange("(t p) c -> p t c", p=P)
    table = nc.dram_tensor("node_table", [N + 1, ROW], fp32, kind="Internal").ap()
    table_tiles = table[0:N, :].rearrange("(t p) c -> p t c", p=P)

    with ExitStack() as stack:
        sb = lambda name, shape, dt: stack.enter_context(nc.sbuf_tensor(name, shape, dt))
        ps = lambda name, shape, dt: stack.enter_context(nc.psum_tensor(name, shape, dt))
        sem = lambda name: stack.enter_context(nc.semaphore(name))

        x_sb = sb("x_sb", [P, TILES, D], fp32)
        h_sb = sb("h_sb", [P, TILES, ROW], fp32)
        adj_sb = sb("adj_sb", [P, LOAD_SLOTS, HALF], i32)
        square = sb("square", [P, 2, HALF], bf16)
        ident = sb("ident", [P, P], fp32)
        bit_ident = sb("bit_ident", [P, BITS, P], bf16)
        bit_mask = sb("bit_mask", [P, BITS], i32)
        code_base = sb("code_base", [P, PAIR, 2, 8, BITS], i32)
        row_id = sb("row_id", [P, TILES], i32)
        offset = sb("offset", [P, P], i32)
        ones = sb("ones", [P, P], fp32)
        W_sb = sb("W_sb", [P, D], fp32)
        WT_sb = sb("WT_sb", [P, D], fp32)
        a_sb = sb("a_sb", [P, 2], fp32)
        W_ext = sb("W_ext", [P, ROW], fp32)
        xT = sb("xT", [P, 2, PRO * P], fp32)
        x_sum = sb("x_sum", [P, PRO_STEPS], fp32)
        x_mean = sb("x_mean", [P, 1], fp32)
        mean_row = sb("mean_row", [1, ROW], fp32)

        half_sum = sb("half_sum", [P, HALVES], fp32)
        top_map = sb("top_map", [P, 2 * PAIR, 8], fp32)
        top_col = sb("top_col", [P, 2 * PAIR, 8], u32)
        top_int = sb("top_int", [P, 2 * PAIR, 8], i32)
        bit_set = sb("bit_set", [P, PAIR, CAND], i32)
        code_all = sb("code_all", [P, PAIR, CAND], fp32)
        cand = sb("cand", [P, PAIR, CAND], fp32)
        cand_rest = sb("cand_rest", [P, PAIR, CAND], fp32)
        code = sb("code", [P, PAIR, 16], fp32)
        is_code = sb("is_code", [P, PAIR, SLOTS], fp32)
        found = sb("found", [P, PAIR], fp32)
        expected = sb("expected", [P, PAIR], fp32)
        cap = sb("cap", [P, GROUPS, PAIR, SLOTS], fp32)
        index = sb("index", [P, GROUPS, PAIR, SLOTS], u32)
        bad = sb("bad", [P, TILES], fp32)

        nb = sb("nb", [P, GROUPS, PAIR, SLOTS, ROW], fp32)
        score = sb("score", [P, PAIR, SLOTS], fp32)
        score_l = sb("score_l", [P, PAIR, SLOTS], fp32)
        score_e = sb("score_e", [P, PAIR, SLOTS], fp32)
        weight = sb("weight", [P, PAIR, SLOTS], fp32)
        row_max = sb("row_max", [P, PAIR], fp32)
        w_sum = sb("w_sum", [P, PAIR], fp32)
        w_inv = sb("w_inv", [P, PAIR], fp32)
        diag = sb("diag", [P, PAIR, SLOTS, P], fp32)
        z = sb("z", [P, PAIR, D], fp32)
        z_neg = sb("z_neg", [P, PAIR, D], fp32)
        z_exp = sb("z_exp", [P, PAIR, D], fp32)
        elu = sb("elu", [P, PAIR, D], fp32)
        y = sb("y", [P, PAIR, D], fp32)
        stats = sb("stats", [P, PAIR, 6], fp32)
        mean_var = sb("mean_var", [P, PAIR, 2], fp32)
        var_eps = sb("var_eps", [P, PAIR], fp32)
        guess_i = sb("guess_i", [P, PAIR], i32)
        rstd = sb("rstd", [P, PAIR], fp32)
        newton = sb("newton", [P, PAIR], fp32)
        newton2 = sb("newton2", [P, PAIR], fp32)
        y_out = sb("y_out", [P, GROUPS, PAIR, D], fp32)

        n_bad_f = sb("n_bad_f", [P, 1], fp32)
        n_bad = sb("n_bad", [1, 1], i32)
        key = sb("key", [P, TILES], fp32)
        key_max = sb("key_max", [P, 1], fp32)
        this_key = sb("this_key", [1, 1], fp32)
        this_row = sb("this_row", [1, 1], i32)
        key_bc = sb("key_bc", [P, 1], fp32)
        adj_row = sb("adj_row", [TILES, P], i32)
        x_row = sb("x_row", [1, D], fp32)
        s_bc = sb("s_bc", [P, 1], fp32)
        mask = sb("mask", [TILES, P], fp32)
        maskT = sb("maskT", [P, TILES], fp32)
        r_score = sb("r_score", [P, TILES], fp32)
        r_lrelu = sb("r_lrelu", [P, TILES], fp32)
        r_neg = sb("r_neg", [P, TILES], fp32)
        r_e = sb("r_e", [P, TILES], fp32)
        r_max = sb("r_max", [P, 1], fp32)
        r_negmax = sb("r_negmax", [1, 1], fp32)
        r_negmax_bc = sb("r_negmax_bc", [P, 1], fp32)
        r_w = sb("r_w", [P, TILES], fp32)
        r_wsum = sb("r_wsum", [P, 1], fp32)
        r_inv = sb("r_inv", [1, 1], fp32)
        r_z = sb("r_z", [1, D], fp32)
        r_zneg = sb("r_zneg", [1, D], fp32)
        r_zexp = sb("r_zexp", [1, D], fp32)
        r_elu = sb("r_elu", [1, D], fp32)
        r_y = sb("r_y", [1, D], fp32)
        r_out = sb("r_out", [1, D], fp32)

        fold = ps("fold", [P, LOAD_SLOTS, FOLD], fp32)
        acc = ps("acc", [P, PAIR, 256], fp32)
        xT_ps = ps("xT_ps", [P, PRO * P], fp32)
        h_ps = ps("h_ps", [P, 2, 2, 256], fp32)

        x_loaded = [sem(f"x_loaded{q}") for q in range(4)]
        weights_loaded = sem("weights_loaded")
        loaded = [sem(f"loaded{s}") for s in range(LOAD_SLOTS)]
        gathered = [sem(f"gathered{g}") for g in range(GROUPS)]
        out_stored = [sem(f"out_stored{g}") for g in range(GROUPS)]
        table_stored = sem("table_stored")
        iotas_ready = sem("iotas_ready")
        v_const = sem("v_const")
        consts_ready = sem("consts_ready")
        w_turned = sem("w_turned")
        wt_ready = sem("wt_ready")
        wa_ready = sem("wa_ready")
        w_ext_ready = sem("w_ext_ready")
        xt_turned = sem("xt_turned")
        xt_ready = sem("xt_ready")
        h_made = sem("h_made")
        h_copied = sem("h_copied")
        x_mean_ready = sem("x_mean_ready")
        mean_made = sem("mean_made")
        mean_ready = sem("mean_ready")
        squared = sem("squared")
        folded = sem("folded")
        picked = sem("picked")
        listed = sem("listed")
        v_front = sem("v_front")
        v_back = sem("v_back")
        scored = sem("scored")
        weighed = sem("weighed")
        diag_ready = sem("diag_ready")
        summed = sem("summed")
        elu_in = sem("elu_in")
        elu_exp = sem("elu_exp")
        out_ready = sem("out_ready")
        bad_counted = sem("bad_counted")
        bad_summed = sem("bad_summed")
        n_bad_ready = sem("n_bad_ready")
        v_row = sem("v_row")
        row_to_pe = sem("row_to_pe")
        pe_to_row = sem("pe_to_row")
        row_picked = sem("row_picked")
        row_loaded = sem("row_loaded")
        row_to_act = sem("row_to_act")
        act_to_row = sem("act_to_row")
        row_done = sem("row_done")
        row_stored = sem("row_stored")
        sp_spare, pool_spare, act_spare, pe_spare, dve_spare = [
            sem(f"{e}_spare") for e in ("sp", "pool", "act", "pe", "dve")]

        def bodies(eng, body):
            body(0, True, False)
            body(1, True, True)
            with eng.Fori(2, BODIES) as i:
                body(i, True, True)
            body(BODIES, False, True)

        first = lambda i: isinstance(i, int) and i == 0

        with nc.Block() as block:

            @block.sync
            def _(sp):
                nc.sync.dma_start(W_sb[:], W).then_inc(weights_loaded, 16)
                with nc.allow_non_contiguous_dma(reason="256 numbers, one per partition"):
                    nc.sync.dma_start(a_sb[:, 0:1], a[D:2 * D, :]).then_inc(weights_loaded, 16)
                    nc.sync.dma_start(a_sb[:, 1:2], a[0:D, :]).then_inc(weights_loaded, 16)
                Q = TILES // 4
                for q in range(4):
                    nc.sync.dma_start(x_sb[:, q * Q:(q + 1) * Q, :],
                                      x_tiles[:, q * Q:(q + 1) * Q, :]).then_inc(x_loaded[q], 16)

                def body(i, front, back):
                    if not front:
                        return
                    for h in range(HALVES):
                        if not (first(i) and h < LOAD_SLOTS):
                            sp.wait_ge(squared, i * HALVES + (h + 1 - LOAD_SLOTS))
                        tile = adj_tiles[bass.ds(i * BODY + h // 2, 1), :, (h % 2) * HALF:(h % 2 + 1) * HALF]
                        nc.sync.dma_start(adj_sb[:, h % LOAD_SLOTS, :], tile.rearrange("o p c -> (o p) c")
                                          ).then_inc(loaded[h % LOAD_SLOTS], 16)
                bodies(sp, body)

                for g in range(GROUPS):
                    sp.wait_ge(out_stored[g], 16 * BODIES)

                sp.wait_ge(n_bad_ready, 1)
                n = sp.value_load(n_bad[0:1, 0:1], min_val=0, max_val=N)
                with sp.If(n > 0):
                    with sp.Fori(0, n) as r:
                        hold(sp, row_picked, r + 1, sp_spare)
                        row = sp.value_load(this_row[0:1, 0:1], min_val=0, max_val=N - 1)
                        nc.sync.dma_start(adj_row[:], adj[bass.ds(row, 1), :].rearrange(
                            "o (c q) -> (o c) q", q=P)).then_inc(row_loaded, 16)
                        nc.sync.dma_start(x_row[:], x[bass.ds(row, 1), :]).then_inc(row_loaded, 16)
                        with nc.allow_non_contiguous_dma(reason="one number to all partitions"):
                            nc.sync.dma_start(s_bc[:], table[bass.ds(row, 1), S_COL:S_COL + 1]
                                              .to_broadcast([P, 1])).then_inc(row_loaded, 16)
                        hold(sp, row_done, r + 1, sp_spare)
                        nc.sync.dma_start(out[bass.ds(row, 1), :], r_out[:]).then_inc(row_stored, 16)
                        hold(sp, row_stored, (r + 1) * 16, sp_spare)

            @block.gpsimd
            def _(pool):
                nc.gpsimd.iota(offset[:], pattern=[[1, P]], base=0, channel_multiplier=-1).then_inc(iotas_ready, 1)
                nc.gpsimd.iota(code_base[:].rearrange("p t h s b -> p (t h) s b"),
                               pattern=[[0, PAIR], [-HALF, 2], [0, 8], [-FOLD, BITS]], base=N,
                               channel_multiplier=0).then_inc(iotas_ready, 1)
                nc.gpsimd.iota(row_id[:], pattern=[[P, TILES]], base=1, channel_multiplier=1).then_inc(iotas_ready, 1)

                with pool.Fori(0, PRO_STEPS) as i:
                    hold(pool, h_copied, i + 1, pool_spare)
                    nc.gpsimd.dma_start(table_tiles[:, bass.ds(i * PRO, PRO), :],
                                        h_sb[:, bass.ds(i * PRO, PRO), :]).then_inc(table_stored, 16)
                pool.wait_ge(mean_ready, 1)
                nc.gpsimd.dma_start(table[N:N + 1, :], mean_row[:]).then_inc(table_stored, 16)
                pool.wait_ge(table_stored, 16 * (PRO_STEPS + 1))
                pool.wait_ge(consts_ready, 1)

                def body(i, front, back):
                    if not front:
                        return
                    for g in range(GROUPS):
                        hold(pool, listed, i * GROUPS + (g + 1), pool_spare)
                        if not first(i):
                            hold(pool, summed, i * GROUPS + (g + 1 - GROUPS), pool_spare)
                        for t in range(PAIR):
                            for k in range(SLOTS):
                                nc.gpsimd.indirect_dma_start(
                                    out=nb[:, g, t, k, :], out_offset=None, in_=table[:, :],
                                    in_offset=bass.IndirectOffsetOnAxis(ap=index[:, g, t, k:k + 1], axis=0),
                                    bounds_check=N if k == 0 else N - 1, oob_is_err=False,
                                ).then_inc(gathered[g], 16)
                bodies(pool, body)

            @block.scalar
            def _(act):
                act.wait_ge(w_turned, 1)
                nc.scalar.copy(WT_sb[:], xT_ps[:, 0:P]).then_inc(wt_ready, 1)
                act.wait_ge(wa_ready, 1)
                nc.scalar.copy(W_ext[:, D:D + 2], xT_ps[:, P:P + 2]).then_inc(w_ext_ready, 1)

                for i in range(PRO_STEPS):
                    act.wait_ge(xt_turned, i + 1)
                    if i >= 2:
                        act.wait_ge(h_made, i - 1)
                    nc.scalar.activation(xT[:, i % 2, :], xT_ps[:], ACT.Copy,
                                         accum_out=x_sum[:, i:i + 1]).then_inc(xt_ready, 1)

                def body(i, front, back):
                    def do_square(g, q):
                        h = g * 2 * PAIR + q
                        act.wait_ge(loaded[h % LOAD_SLOTS], i * (16 * HALVES // LOAD_SLOTS)
                                    + 16 * (h // LOAD_SLOTS + 1))
                        if not (first(i) and h < 2):
                            act.wait_ge(folded, i * HALVES + (h - 1))
                        if q == 0 and not first(i):
                            act.wait_ge(listed, i * GROUPS + (g + 1 - GROUPS))
                        nc.scalar.activation(square[:, h % 2, :], adj_sb[:, h % LOAD_SLOTS, :], ACT.Square,
                                             accum_out=half_sum[:, h:h + 1]).then_inc(squared, 1)

                    def store(i_of, g):
                        act.wait_ge(out_ready, i_of * GROUPS + (g + 1))
                        nc.scalar.dma_start(out_tiles[:, bass.ds(i_of * BODY + g * PAIR, PAIR), :],
                                            y_out[:, g, :, :]).then_inc(out_stored[g], 16)

                    for g in range(GROUPS):
                        if front:
                            do_square(g, 0)
                            do_square(g, 1)
                        if back:
                            if g > 0:
                                store(i - 1, g - 1)
                            elif not (isinstance(i, int) and i == 1):
                                store(i - 2, GROUPS - 1)
                            act.wait_ge(scored, (i - 1) * GROUPS + (g + 1))
                            nc.scalar.activation(weight[:], score_e[:], ACT.Exp).then_inc(weighed, 1)
                        if front:
                            do_square(g, 2)
                            do_square(g, 3)
                        if back:
                            act.wait_ge(elu_in, (i - 1) * GROUPS + (g + 1))
                            nc.scalar.activation(z_exp[:], z_neg[:], ACT.Exp).then_inc(elu_exp, 1)
                    if not front:
                        store(i - 1, GROUPS - 1)
                bodies(act, body)

                act.wait_ge(n_bad_ready, 1)
                n = act.value_load(n_bad[0:1, 0:1], min_val=0, max_val=N)
                with act.If(n > 0):
                    with act.Fori(0, n) as r:
                        hold(act, row_to_act, r * 2 + 1, act_spare)
                        nc.scalar.activation(r_w[:], r_e[:], ACT.Exp, bias=r_negmax_bc[:, 0:1],
                                             accum_out=r_wsum[:]).then_inc(act_to_row, 1)
                        hold(act, row_to_act, r * 2 + 2, act_spare)
                        nc.scalar.activation(r_zexp[:], r_zneg[:], ACT.Exp).then_inc(act_to_row, 1)

            @block.tensor
            def _(pe):
                pe.wait_ge(weights_loaded, 48)
                pe.wait_ge(consts_ready, 1)
                nc.tensor.transpose(xT_ps[:, 0:P], W_sb[:], ident[:]).then_inc(w_turned, 1)
                pe.wait_ge(wt_ready, 1)
                nc.tensor.matmul(xT_ps[:, P:P + 2], WT_sb[:], a_sb[:], start=True, stop=True).then_inc(wa_ready, 1)
                pe.wait_ge(w_ext_ready, 2)

                for i in range(PRO_STEPS):
                    if i % (PRO_STEPS // 4) == 0:
                        pe.wait_ge(x_loaded[i // (PRO_STEPS // 4)], 16)
                    if i >= 1:
                        pe.wait_ge(xt_ready, i)
                    for q in range(PRO):
                        last = nc.tensor.transpose(xT_ps[:, q * P:(q + 1) * P], x_sb[:, i * PRO + q, :], ident[:])
                    last.then_inc(xt_turned, 1)
                    pe.wait_ge(xt_ready, i + 1)
                    if i >= 1:
                        pe.wait_ge(h_copied, i)
                    for q in range(PRO):
                        last = nc.tensor.matmul(h_ps[:, q // 2, q % 2, 0:ROW], xT[:, i % 2, q * P:(q + 1) * P],
                                                W_ext[:], start=True, stop=True)
                    last.then_inc(h_made, 1)
                pe.wait_ge(x_mean_ready, 1)
                pe.wait_ge(h_copied, PRO_STEPS)
                nc.tensor.matmul(h_ps[0:1, 0, 0, 0:ROW], x_mean[:], W_ext[:], start=True, stop=True
                                 ).then_inc(mean_made, 1)

                def body(i, front, back):
                    def do_fold(g, q):
                        h = g * 2 * PAIR + q
                        pe.wait_ge(squared, i * HALVES + (h + 1))
                        if not (first(i) and h < LOAD_SLOTS):
                            pe.wait_ge(picked, i * HALVES + (h + 1 - LOAD_SLOTS))
                        for b in range(BITS):
                            last = nc.tensor.matmul(fold[:, h % LOAD_SLOTS, :], bit_ident[:, b, :],
                                                    square[:, h % 2, b * FOLD:(b + 1) * FOLD],
                                                    start=b == 0, stop=b == BITS - 1)
                        last.then_inc(folded, 1)

                    for g in range(GROUPS):
                        if front:
                            do_fold(g, 0)
                            do_fold(g, 1)
                            do_fold(g, 2)
                        if back:
                            pe.wait_ge(diag_ready, (i - 1) * GROUPS + (g + 1))
                            for t in range(PAIR):
                                for k in range(SLOTS):
                                    last = nc.tensor.matmul(acc[:, t, 0:D], diag[:, t, k, :], nb[:, g, t, k, 0:D],
                                                            start=k == 0, stop=k == SLOTS - 1)
                            last.then_inc(summed, 1)
                        if front:
                            do_fold(g, 3)
                bodies(pe, body)

                pe.wait_ge(bad_counted, 1)
                nc.tensor.matmul(xT_ps[0:1, 0:1], n_bad_f[:], ones[:, 0:1], start=True, stop=True
                                 ).then_inc(bad_summed, 1)
                pe.wait_ge(n_bad_ready, 1)
                n = pe.value_load(n_bad[0:1, 0:1], min_val=0, max_val=N)
                with pe.If(n > 0):
                    with pe.Fori(0, n) as r:
                        hold(pe, row_to_pe, r * 4 + 1, pe_spare)
                        nc.tensor.transpose(xT_ps[0:1, 0:P], key_max[:], ident[:]).then_inc(pe_to_row, 1)
                        hold(pe, row_picked, r + 1, pe_spare)
                        nc.tensor.matmul(xT_ps[:, P:P + 1], ones[0:1, :], this_key[:], start=True, stop=True
                                         ).then_inc(pe_to_row, 1)
                        hold(pe, row_to_pe, r * 4 + 2, pe_spare)
                        nc.tensor.transpose(xT_ps[:, 2 * P:2 * P + TILES], mask[:], ident[0:TILES, 0:TILES]
                                            ).then_inc(pe_to_row, 1)
                        hold(pe, row_to_pe, r * 4 + 3, pe_spare)
                        nc.tensor.transpose(xT_ps[0:1, 0:P], r_max[:], ident[:]).then_inc(pe_to_row, 1)
                        hold(pe, row_to_pe, r * 4 + 4, pe_spare)
                        nc.tensor.matmul(xT_ps[:, P:P + 1], ones[0:1, :], r_negmax[:], start=True, stop=True
                                         ).then_inc(pe_to_row, 1)
                        hold(pe, act_to_row, r * 2 + 1, pe_spare)
                        nc.tensor.matmul(xT_ps[0:1, 0:1], r_wsum[:], ones[:, 0:1], start=True, stop=True)
                        for c in range(TILES):
                            last = nc.tensor.matmul(h_ps[0:1, 0, 0, 0:D], r_w[:, c:c + 1], h_sb[:, c, 0:D],
                                                    start=c == 0, stop=c == TILES - 1)
                        last.then_inc(pe_to_row, 1)
                        hold(pe, row_done, r + 1, pe_spare)

            @block.vector
            def _(dve):
                s = Steps(dve, v_const)
                nc.vector.memset(nb[:], 0.0)
                nc.vector.memset(ones[:], 1.0)
                for b in range(BITS):
                    nc.vector.memset(bit_mask[:, b:b + 1], 1 << b)
                dve.wait_ge(iotas_ready, 3)
                s.after(nc.vector.tensor_scalar(ident[:], offset[:], 0.0, None, ALU.is_equal))
                for b in range(BITS):
                    last = nc.vector.tensor_scalar(bit_ident[:, b, :], ident[:], float(1 << b), None, ALU.mult)
                s.after(last)
                nc.vector.memset(n_bad_f[:], 0.0).then_inc(consts_ready, 1)
                dve.wait_ge(weights_loaded, 48)
                nc.vector.tensor_copy(W_ext[:, 0:D], W_sb[:]).then_inc(w_ext_ready, 1)

                with dve.Fori(0, PRO_STEPS) as i:
                    hold(dve, h_made, i + 1, dve_spare)
                    nc.vector.tensor_copy(
                        h_sb[:, bass.ds(i * PRO, PRO), :].rearrange("p (u v) c -> p u v c", v=2),
                        h_ps[:, :, :, 0:ROW]).then_inc(h_copied, 1)
                dve.wait_ge(xt_ready, PRO_STEPS)
                s.after(nc.vector.reduce_sum(n_bad_f[:], x_sum[:], AX.X))
                nc.vector.tensor_scalar(x_mean[:], n_bad_f[:], 1.0 / N, None, ALU.mult).then_inc(x_mean_ready, 1)
                dve.wait_ge(mean_made, 1)
                nc.vector.tensor_copy(mean_row[:], h_ps[0:1, 0, 0, 0:ROW]).then_inc(mean_ready, 1)

                def body(i, front, back):
                    for g in range(GROUPS):
                        if front:
                            dve.sem_clear(v_front)
                        if back:
                            dve.sem_clear(v_back)
                        f, v = Steps(dve, v_front), Steps(dve, v_back)
                        n = (i - 1) * GROUPS + (g + 1)

                        def pick(q):
                            h = g * 2 * PAIR + q
                            hold(dve, folded, i * HALVES + (h + 1), dve_spare)
                            f.after(nc.vector.max(top_map[:, q, :], fold[:, h % LOAD_SLOTS, :]))
                            nc.vector.max_index(top_col[:, q, :], top_map[:, q, :], fold[:, h % LOAD_SLOTS, :]
                                                ).then_inc(picked, 1)

                        def lists():
                            cols = [P, 2 * PAIR * 8, BITS]
                            split = lambda t: t.rearrange("p t (c b) -> p (t c) b", b=BITS)
                            dve.wait_ge(picked, i * HALVES + (g + 1) * 2 * PAIR)
                            f.after(nc.vector.tensor_copy(top_int[:], top_map[:]))
                            nc.vector.tensor_tensor(
                                split(bit_set[:]),
                                top_int[:].rearrange("p q s -> p (q s)").unsqueeze(2).to_broadcast(cols),
                                bit_mask[:].unsqueeze(1).to_broadcast(cols), ALU.bitwise_and)
                            f.after(nc.vector.tensor_tensor(
                                split(code_all[:]), code_base[:].rearrange("p t h s b -> p (t h s) b"),
                                top_col[:].rearrange("p q s -> p (q s)").unsqueeze(2).to_broadcast(cols),
                                ALU.subtract))
                            f.after(nc.vector.scalar_tensor_tensor(cand[:], bit_set[:], 0.0, code_all[:],
                                                                   ALU.is_gt, ALU.mult))
                            for t in range(PAIR):
                                f.after(nc.vector.max(code[:, t, 0:8], cand[:, t, :]))
                                f.after(nc.vector.match_replace(cand_rest[:, t, :], code[:, t, 0:8],
                                                                cand[:, t, :], 0.0))
                                last = nc.vector.max(code[:, t, 8:16], cand_rest[:, t, :])
                            f.after(last)
                            if not first(i):
                                dve.wait_ge(gathered[g], i * (16 * PAIR * SLOTS))
                            nc.vector.tensor_scalar(index[:, g, :, :], code[:, :, 0:SLOTS], -1.0, float(N),
                                                    ALU.mult, ALU.add)
                            nc.vector.tensor_scalar(cap[:, g, :, :], code[:, :, 0:SLOTS], 1e30, NEG,
                                                    ALU.mult, ALU.add)
                            nc.vector.tensor_tensor(
                                expected[:], half_sum[:, g * 2 * PAIR:(g + 1) * 2 * PAIR:2],
                                half_sum[:, g * 2 * PAIR + 1:(g + 1) * 2 * PAIR:2], ALU.add)
                            f.after(nc.vector.tensor_scalar(is_code[:], code[:, :, 0:SLOTS], 0.0, None, ALU.is_gt))
                            f.after(nc.vector.reduce_sum(found[:], is_code[:], AX.X))
                            nc.vector.tensor_tensor(bad[:, bass.ds(i * BODY + g * PAIR, PAIR)], found[:],
                                                    expected[:], ALU.not_equal).then_inc(listed, 1)

                        def scores():
                            dve.wait_ge(gathered[g], i * (16 * PAIR * SLOTS))
                            slots = [P, PAIR, SLOTS]
                            mine = bass.ds((i - 1) * BODY + g * PAIR, PAIR)
                            v.after(nc.vector.tensor_tensor(score[:], nb[:, g, :, :, T_COL],
                                                            h_sb[:, mine, S_COL:S_COL + 1].to_broadcast(slots),
                                                            ALU.add))
                            v.after(nc.vector.scalar_tensor_tensor(score_l[:], score[:], ALPHA, score[:],
                                                                   ALU.mult, ALU.max))
                            v.after(nc.vector.tensor_tensor(score_l[:, :, 1:SLOTS], score_l[:, :, 1:SLOTS],
                                                            cap[:, g, :, 1:SLOTS], ALU.min))
                            v.after(nc.vector.reduce_max(row_max[:], score_l[:], AX.X))
                            nc.vector.tensor_tensor(score_e[:], score_l[:],
                                                    row_max[:].unsqueeze(2).to_broadcast(slots),
                                                    ALU.subtract).then_inc(scored, 1)

                        def weights():
                            dve.wait_ge(weighed, n)
                            big = [P, PAIR * SLOTS, P]
                            nc.vector.tensor_tensor(
                                diag[:].rearrange("p t k c -> p (t k) c"),
                                ident[:].unsqueeze(1).to_broadcast(big),
                                weight[:].rearrange("p t k -> p (t k)").unsqueeze(2).to_broadcast(big),
                                ALU.mult).then_inc(diag_ready, 1)
                            v.after(nc.vector.reduce_sum(w_sum[:], weight[:], AX.X))
                            v.after(nc.vector.reciprocal(w_inv[:], w_sum[:]))

                        def divide():
                            dve.wait_ge(summed, n)
                            v.after(nc.vector.tensor_tensor(z[:], acc[:, :, 0:D],
                                                            w_inv[:].unsqueeze(2).to_broadcast([P, PAIR, D]),
                                                            ALU.mult))
                            nc.vector.tensor_scalar(z_neg[:], z[:], 0.0, None, ALU.min).then_inc(elu_in, 1)

                        def finish():
                            dve.wait_ge(elu_exp, n)
                            v.after(nc.vector.scalar_tensor_tensor(elu[:], z[:], 0.0, z_exp[:], ALU.max, ALU.add))
                            mine = bass.ds((i - 1) * BODY + g * PAIR, PAIR)
                            v.after(nc.vector.scalar_tensor_tensor(y[:], elu[:], -1.0, x_sb[:, mine, :],
                                                                   ALU.add, ALU.add))
                            norm(v, y, [(y[:, t, :], stats[:, t, :], mean_var[:, t, :]) for t in range(PAIR)],
                                 mean_var[:, :, 1], var_eps[:], guess_i[:], rstd[:], newton[:], newton2[:])
                            if not (isinstance(i, int) and i == 1):
                                dve.wait_ge(out_stored[g], (i - 1) * 16)
                            for t in range(PAIR):
                                last = nc.vector.tensor_scalar(y_out[:, g, t, :], y[:, t, :],
                                                               mean_var[:, t, 0:1], rstd[:, t:t + 1],
                                                               ALU.subtract, ALU.mult)
                            last.then_inc(out_ready, 1)

                        if front:
                            pick(0)
                        if back:
                            scores()
                        if front:
                            pick(1)
                        if back:
                            weights()
                        if front:
                            pick(2)
                        if back:
                            divide()
                        if front:
                            pick(3)
                            lists()
                        if back:
                            finish()

                def norm(v, y, parts, var, var_e, guess, inv, t1, t2):
                    for part, st, mv in parts:
                        last = nc.vector.bn_stats(st, part)
                    v.after(last)
                    for part, st, mv in parts:
                        last = nc.vector.bn_aggr(mv, st)
                    v.after(last)
                    v.after(nc.vector.tensor_scalar(var_e, var, EPS, None, ALU.add))
                    v.after(nc.vector.tensor_scalar(guess, var_e.bitcast(i32), 1, None, ALU.logical_shift_right))
                    v.after(nc.vector.tensor_scalar(inv.bitcast(i32), guess, -1.0, float(0x5f3759df),
                                                    ALU.mult, ALU.add))
                    for _ in range(3):
                        v.after(nc.vector.tensor_tensor(t1, inv, inv, ALU.mult))
                        v.after(nc.vector.scalar_tensor_tensor(t2, t1, -0.5, var_e, ALU.mult, ALU.mult))
                        v.after(nc.vector.scalar_tensor_tensor(inv, t2, 1.5, inv, ALU.add, ALU.mult))

                bodies(dve, body)

                dve.wait_ge(listed, BODIES * GROUPS)
                nc.vector.tensor_tensor(key[:], bad[:], row_id[:], ALU.mult)
                nc.vector.reduce_sum(n_bad_f[:], bad[:], AX.X).then_inc(bad_counted, 1)
                dve.wait_ge(bad_summed, 1)
                nc.vector.tensor_copy(n_bad[:], xT_ps[0:1, 0:1]).then_inc(n_bad_ready, 1)
                dve.wait_ge(n_bad_ready, 1)
                n = dve.value_load(n_bad[0:1, 0:1], min_val=0, max_val=N)
                with dve.If(n > 0):
                    with dve.Fori(0, n) as r:
                        dve.sem_clear(v_row)
                        v = Steps(dve, v_row)
                        nc.vector.reduce_max(key_max[:], key[:], AX.X).then_inc(row_to_pe, 1)
                        hold(dve, pe_to_row, r * 6 + 1, dve_spare)
                        v.after(nc.vector.reduce_max(this_key[:], xT_ps[0:1, 0:P], AX.X))
                        nc.vector.tensor_scalar(this_row[:], this_key[:], -1.0, None, ALU.add).then_inc(row_picked, 1)
                        hold(dve, pe_to_row, r * 6 + 2, dve_spare)
                        v.after(nc.vector.tensor_copy(key_bc[:], xT_ps[:, P:P + 1]))
                        v.after(nc.vector.scalar_tensor_tensor(key[:], key[:], key_bc[:, 0:1], key[:],
                                                               ALU.is_lt, ALU.mult))
                        hold(dve, row_loaded, (r + 1) * 48, dve_spare)
                        nc.vector.tensor_scalar(mask[:], adj_row[:], 0.0, None, ALU.is_gt).then_inc(row_to_pe, 1)
                        v.after(nc.vector.tensor_scalar(r_score[:], h_sb[:, :, T_COL], s_bc[:, 0:1], None, ALU.add))
                        nc.vector.scalar_tensor_tensor(r_lrelu[:], r_score[:], ALPHA, r_score[:], ALU.mult, ALU.max)
                        hold(dve, pe_to_row, r * 6 + 3, dve_spare)
                        v.after(nc.vector.tensor_copy(maskT[:], xT_ps[:, 2 * P:2 * P + TILES]))
                        nc.vector.tensor_scalar(r_neg[:], maskT[:], -NEG, NEG, ALU.mult, ALU.add)
                        v.after(nc.vector.tensor_tensor(r_e[:], r_lrelu[:], maskT[:], ALU.mult))
                        v.after(nc.vector.tensor_tensor(r_e[:], r_e[:], r_neg[:], ALU.add))
                        nc.vector.reduce_max(r_max[:], r_e[:], AX.X).then_inc(row_to_pe, 1)
                        hold(dve, pe_to_row, r * 6 + 4, dve_spare)
                        nc.vector.tensor_reduce(r_negmax[:], xT_ps[0:1, 0:P], AX.X, ALU.max, negate=True
                                                ).then_inc(row_to_pe, 1)
                        hold(dve, pe_to_row, r * 6 + 5, dve_spare)
                        nc.vector.tensor_copy(r_negmax_bc[:], xT_ps[:, P:P + 1]).then_inc(row_to_act, 1)
                        hold(dve, pe_to_row, r * 6 + 6, dve_spare)
                        v.after(nc.vector.reciprocal(r_inv[:], xT_ps[0:1, 0:1]))
                        v.after(nc.vector.tensor_scalar(r_z[:], h_ps[0:1, 0, 0, 0:D], r_inv[:, 0:1], None, ALU.mult))
                        nc.vector.tensor_scalar(r_zneg[:], r_z[:], 0.0, None, ALU.min).then_inc(row_to_act, 1)
                        hold(dve, act_to_row, r * 2 + 2, dve_spare)
                        v.after(nc.vector.scalar_tensor_tensor(r_elu[:], r_z[:], 0.0, r_zexp[:], ALU.max, ALU.add))
                        v.after(nc.vector.scalar_tensor_tensor(r_y[:], r_elu[:], -1.0, x_row[:], ALU.add, ALU.add))
                        norm(v, r_y, [(r_y[:], stats[0:1, 0, :], mean_var[0:1, 0, :])], mean_var[0:1, 0, 1:2],
                             var_eps[0:1, 0:1], guess_i[0:1, 0:1], rstd[0:1, 0:1], newton[0:1, 0:1],
                             newton2[0:1, 0:1])
                        nc.vector.tensor_scalar(r_out[:], r_y[:], mean_var[0:1, 0, 0:1], rstd[0:1, 0:1],
                                                ALU.subtract, ALU.mult).then_inc(row_done, 1)
                        hold(dve, row_stored, (r + 1) * 16, dve_spare)


_INS = ['x', 'adj', 'L0_gnn_W', 'L0_gnn_a']
_OUTS = [((8192, 128), 'float32')]


def kernel(**inputs):
    import numpy as _np
    import concourse.bacc as _bacc
    from concourse import mybir as _mybir
    from concourse.bass_utils import run_bass_kernel_spmd as _run

    nc = _bacc.Bacc("TRN2", target_bir_lowering=False, num_devices=1)
    arrays, args = {}, []
    for name in _INS:
        a = _np.ascontiguousarray(inputs[name])
        arrays[f"in_{name}"] = a
        args.append(nc.dram_tensor(f"in_{name}", a.shape, _mybir.dt.from_np(a.dtype), kind="ExternalInput").ap())
    for i, (shape, dtype) in enumerate(_OUTS):
        dt = _mybir.dt.from_np(_np.dtype(dtype))
        args.append(nc.dram_tensor(f"out_{i}", shape, dt, kind="ExternalOutput").ap())
    graph_attention(nc, *args)
    r = _run(nc, [arrays], core_ids=[0])
    return r.results[0]["out_0"]
```

```python
from contextlib import ExitStack

import concourse.bass as bass
from concourse import mybir

SLOTS = 10
CHUNKS = 3
NEG = -9000000000000000.0
ALPHA = 0.2
EPS = 1e-5


class Steps:

    def __init__(self, eng, sem):
        self.eng, self.sem, self.n = eng, sem, 0

    def after(self, instruction):
        self.n += 1
        instruction.then_inc(self.sem, 1)
        self.eng.wait_ge(self.sem, self.n)


def hold(eng, sem, value, spare):
    eng.wait_ge(sem, value)
    eng.sem_inc(spare, 1)


def graph_attention(nc, x, adj, W, a, out):
    fp32, i32, u32, bf16 = mybir.dt.float32, mybir.dt.int32, mybir.dt.uint32, mybir.dt.bfloat16
    ACT, ALU, AX = mybir.ActivationFunctionType, mybir.AluOpType, mybir.AxisListType

    N, D = x.shape
    P = 128
    assert D == P and adj.shape[0] == N and adj.shape[1] == N
    TILES = N // P
    EDGES = CHUNKS * P
    HALF = N // 2
    BITS = 8
    FOLD = HALF // BITS
    assert FOLD == 512
    PAIR = 2
    GROUPS = 2
    BODY = PAIR * GROUPS
    BODIES = TILES // BODY
    HALVES = 2 * BODY
    LOAD_SLOTS = 4
    SQUARES = 4
    CAND = 2 * 8 * BITS
    PC = PAIR * CHUNKS
    ROW_COL, START_COL = SLOTS, SLOTS + 1
    SENT = SLOTS + 2

    adj_tiles = adj.rearrange("(t p) c -> t p c", p=P)
    out_tiles = out.rearrange("(t p) c -> p t c", p=P)
    x_tiles = x.rearrange("(t p) c -> p t c", p=P)

    with ExitStack() as stack:
        sb = lambda name, shape, dt: stack.enter_context(nc.sbuf_tensor(name, shape, dt))
        ps = lambda name, shape, dt: stack.enter_context(nc.psum_tensor(name, shape, dt))
        sem = lambda name: stack.enter_context(nc.semaphore(name))

        x_sb = sb("x_sb", [P, TILES, D], fp32)
        adj_sb = sb("adj_sb", [P, LOAD_SLOTS, HALF], i32)
        square = sb("square", [P, SQUARES, HALF], bf16)
        ident = sb("ident", [P, P], fp32)
        bit_ident = sb("bit_ident", [P, BITS, P], bf16)
        bit_mask = sb("bit_mask", [P, BITS], i32)
        code_base = sb("code_base", [P, PAIR, 2, 8, BITS], i32)
        row_id = sb("row_id", [P, TILES], i32)
        offset = sb("offset", [P, P], i32)
        before = sb("before", [P, P], fp32)
        edge_iota = sb("edge_iota", [P, EDGES], i32)
        edge_id = sb("edge_id", [P, PC], i32)
        row_iota = sb("row_iota", [P, P], i32)
        slot_iota = sb("slot_iota", [P, SLOTS], i32)
        ones = sb("ones", [P, P], fp32)
        W_sb = sb("W_sb", [P, D], fp32)
        WT_sb = sb("WT_sb", [P, D], fp32)
        a_sb = sb("a_sb", [P, 2], fp32)
        a_bc = sb("a_bc", [P, 2, P], fp32)
        wa_bc = sb("wa_bc", [P, 2, D], fp32)
        x_mean = sb("x_mean", [P, 1], fp32)
        x_mean_bc = sb("x_mean_bc", [P, P], fp32)
        s_all = sb("s_all", [P, TILES], fp32)
        eps_all = sb("eps_all", [P, PAIR], fp32)
        minus_half = sb("minus_half", [P, PAIR], fp32)
        minus_one = sb("minus_one", [P, PAIR], fp32)

        half_sum = sb("half_sum", [P, HALVES], fp32)
        top_map = sb("top_map", [P, 2 * PAIR, 8], fp32)
        top_col = sb("top_col", [P, 2 * PAIR, 8], u32)
        top_int = sb("top_int", [P, 2 * PAIR, 8], i32)
        bit_set = sb("bit_set", [P, PAIR, CAND], i32)
        code_all = sb("code_all", [P, PAIR, CAND], fp32)
        cand = sb("cand", [P, PAIR, CAND], fp32)
        cand_rest = sb("cand_rest", [P, PAIR, CAND], fp32)
        code = sb("code", [P, PAIR, 16], fp32)
        is_code = sb("is_code", [P, PAIR, SLOTS], fp32)
        found = sb("found", [P, PAIR], fp32)
        expected = sb("expected", [P, PAIR], fp32)
        short = sb("short", [P, PAIR], fp32)
        ends = sb("ends", [P, PAIR], fp32)
        half_len = sb("half_len", [P, PAIR], fp32)
        to_middle = sb("to_middle", [P, PAIR], fp32)
        middle = sb("middle", [P, PAIR], fp32)
        from_middle = sb("from_middle", [P, PAIR, EDGES], fp32)
        over = sb("over", [P, PAIR], fp32)
        bad = sb("bad", [P, TILES], fp32)
        cap = sb("cap", [P, GROUPS, PAIR, SLOTS], fp32)
        empty = sb("empty", [P, GROUPS, PAIR], fp32)
        sent = sb("sent", [P, PAIR, SENT], fp32)
        row_edge = sb("row_edge", [P, GROUPS, PAIR, EDGES], fp32)
        edge_in = sb("edge_in", [P, PC, SENT], fp32)
        slot_of = sb("slot_of", [P, PC], fp32)
        at_slot = sb("at_slot", [P, GROUPS, PC, SLOTS], fp32)
        own_code = sb("own_code", [P, PC, SLOTS], fp32)
        edge_code = sb("edge_code", [P, PC], fp32)
        index = sb("index", [P, GROUPS, PC], u32)
        edge_row = sb("edge_row", [P, GROUPS, PC, P], fp32)

        nb = sb("nb", [P, GROUPS, PC, D], fp32)
        dot = sb("dot", [P, PC, D], fp32)
        t_edge = sb("t_edge", [P, PC], fp32)
        t_slot = sb("t_slot", [P, PC, SLOTS], fp32)
        score = sb("score", [P, PAIR, SLOTS], fp32)
        score_l = sb("score_l", [P, PAIR, SLOTS], fp32)
        score_e = sb("score_e", [P, PAIR, SLOTS], fp32)
        weight = sb("weight", [P, PAIR, SLOTS], fp32)
        share = sb("share", [P, PAIR, SLOTS], fp32)
        row_max = sb("row_max", [P, PAIR], fp32)
        w_sum = sb("w_sum", [P, PAIR], fp32)
        w_inv = sb("w_inv", [P, PAIR], fp32)
        own_share = sb("own_share", [P, PC, SLOTS], fp32)
        edge_w = sb("edge_w", [P, PC], fp32)
        spread = sb("spread", [P, PC, P], fp32)
        x_att = sb("x_att", [P, PAIR, P], fp32)
        empty_diag = sb("empty_diag", [P, PAIR, P], fp32)
        z_one = sb("z_one", [P, PAIR, D], fp32)
        z_exp = sb("z_exp", [P, PAIR, D], fp32)
        elu = sb("elu", [P, PAIR, D], fp32)
        y = sb("y", [P, PAIR, D], fp32)
        stats = sb("stats", [P, PAIR, 6], fp32)
        mean_var = sb("mean_var", [P, PAIR, 2], fp32)
        var_eps = sb("var_eps", [P, PAIR], fp32)
        guess_i = sb("guess_i", [P, PAIR], i32)
        rstd = sb("rstd", [P, PAIR], fp32)
        scaled_mean = sb("scaled_mean", [P, PAIR], fp32)
        shift = sb("shift", [P, PAIR], fp32)
        newton = sb("newton", [P, PAIR], fp32)
        newton2 = sb("newton2", [P, PAIR], fp32)
        y_out = sb("y_out", [P, GROUPS, PAIR, D], fp32)

        n_bad_f = sb("n_bad_f", [P, 1], fp32)
        n_bad = sb("n_bad", [1, 1], i32)
        key = sb("key", [P, TILES], fp32)
        key_max = sb("key_max", [P, 1], fp32)
        this_key = sb("this_key", [1, 1], fp32)
        this_row = sb("this_row", [1, 1], i32)
        key_bc = sb("key_bc", [P, 1], fp32)
        adj_row = sb("adj_row", [TILES, P], i32)
        x_row = sb("x_row", [1, D], fp32)
        t_all = sb("t_all", [P, TILES], fp32)
        x_dot = sb("x_dot", [1, D], fp32)
        r_s = sb("r_s", [1, 1], fp32)
        s_bc = sb("s_bc", [P, 1], fp32)
        r_x = sb("r_x", [P, 1], fp32)
        mask = sb("mask", [TILES, P], fp32)
        maskT = sb("maskT", [P, TILES], fp32)
        r_score = sb("r_score", [P, TILES], fp32)
        r_lrelu = sb("r_lrelu", [P, TILES], fp32)
        r_neg = sb("r_neg", [P, TILES], fp32)
        r_e = sb("r_e", [P, TILES], fp32)
        r_max = sb("r_max", [P, 1], fp32)
        r_negmax = sb("r_negmax", [1, 1], fp32)
        r_negmax_bc = sb("r_negmax_bc", [P, 1], fp32)
        r_w = sb("r_w", [P, TILES], fp32)
        r_wsum = sb("r_wsum", [P, 1], fp32)
        r_inv = sb("r_inv", [1, 1], fp32)
        r_z = sb("r_z", [1, D], fp32)
        r_zneg = sb("r_zneg", [1, D], fp32)
        r_zexp = sb("r_zexp", [1, D], fp32)
        r_elu = sb("r_elu", [1, D], fp32)
        r_y = sb("r_y", [1, D], fp32)
        r_out = sb("r_out", [1, D], fp32)

        fold = ps("fold", [P, LOAD_SLOTS, FOLD], fp32)
        small = ps("small", [P, 512], fp32)
        x_att_ps = ps("x_att_ps", [P, PAIR, 256], fp32)
        h_ps = ps("h_ps", [P, PAIR, 256], fp32)
        misc = ps("misc", [P, 512], fp32)
        starts_ps = small[:, 0:PAIR]
        edge_in_ps = small[:, 64:64 + PC * SENT].rearrange("p (c k) -> p c k", k=SENT)
        t_row_ps = misc[:, 192:192 + PAIR * SLOTS].rearrange("p (t k) -> p t k", k=SLOTS)
        share_ps = small[:, 256:256 + PC * SLOTS].rearrange("p (c k) -> p c k", k=SLOTS)

        x_loaded = [sem(f"x_loaded{q}") for q in range(4)]
        weights_loaded = sem("weights_loaded")
        loaded = [sem(f"loaded{s}") for s in range(LOAD_SLOTS)]
        gathered = [sem(f"gathered{g}") for g in range(GROUPS)]
        out_stored = [sem(f"out_stored{g}") for g in range(GROUPS)]
        iotas_ready = sem("iotas_ready")
        v_const = sem("v_const")
        consts_ready = sem("consts_ready")
        w_turned = sem("w_turned")
        wt_ready = sem("wt_ready")
        wa_made = sem("wa_made")
        x_summed = sem("x_summed")
        x_mean_ready = sem("x_mean_ready")
        x_mean_turned = sem("x_mean_turned")
        squared = sem("squared")
        folded = sem("folded")
        picked = sem("picked")
        listed = sem("listed")
        v_step = sem("v_step")
        starts_made = sem("starts_made")
        routed = sem("routed")
        edges_filled = sem("edges_filled")
        indexed = sem("indexed")
        edge_in_ready = sem("edge_in_ready")
        edge_row_made = sem("edge_row_made")
        edge_w_ready = sem("edge_w_ready")
        stats_ready = sem("stats_ready")
        p_step = sem("p_step")
        norm_ready = sem("norm_ready")
        scaled = sem("scaled")
        s_ready = sem("s_ready")
        middle_ready = sem("middle_ready")
        from_middle_made = sem("from_middle_made")
        t_ready = sem("t_ready")
        t_sent = sem("t_sent")
        scored = sem("scored")
        weighed = sem("weighed")
        shared = sem("shared")
        share_sent = sem("share_sent")
        spread_ready = sem("spread_ready")
        summed = sem("summed")
        x_att_ready = sem("x_att_ready")
        h_made = sem("h_made")
        elu_exp = sem("elu_exp")
        bad_counted = sem("bad_counted")
        bad_summed = sem("bad_summed")
        n_bad_ready = sem("n_bad_ready")
        v_rows = sem("v_rows")
        v_row = sem("v_row")
        row_to_pe = sem("row_to_pe")
        pe_to_row = sem("pe_to_row")
        row_picked = sem("row_picked")
        row_loaded = sem("row_loaded")
        row_to_act = sem("row_to_act")
        act_to_row = sem("act_to_row")
        row_done = sem("row_done")
        row_stored = sem("row_stored")
        sp_spare, pool_spare, act_spare, pe_spare, dve_spare = [
            sem(f"{e}_spare") for e in ("sp", "pool", "act", "pe", "dve")]

        def stage(i, g, k):
            j, place = i - (k - g + 1) // GROUPS, (g - k) % GROUPS
            return None if isinstance(j, int) and not 0 <= j < BODIES else (j, place)

        def bodies(eng, body):
            for i in range(3):
                body(i)
            with eng.Fori(3, BODIES) as i:
                body(i)
            for i in range(BODIES, BODIES + 2):
                body(i)

        first = lambda j: isinstance(j, int) and j == 0
        count = lambda j, g: j * GROUPS + (g + 1)

        with nc.Block() as block:

            @block.sync
            def _(sp):
                nc.sync.dma_start(W_sb[:], W).then_inc(weights_loaded, 16)
                with nc.allow_non_contiguous_dma(reason="256 numbers, one per partition"):
                    nc.sync.dma_start(a_sb[:, 0:1], a[D:2 * D, :]).then_inc(weights_loaded, 16)
                    nc.sync.dma_start(a_sb[:, 1:2], a[0:D, :]).then_inc(weights_loaded, 16)
                Q = TILES // 4
                for q in range(4):
                    nc.sync.dma_start(x_sb[:, q * Q:(q + 1) * Q, :],
                                      x_tiles[:, q * Q:(q + 1) * Q, :]).then_inc(x_loaded[q], 16)

                def body(i):
                    if not stage(i, 0, 0):
                        return
                    for h in range(HALVES):
                        if not (first(i) and h < LOAD_SLOTS):
                            sp.wait_ge(squared, i * HALVES + (h + 1 - LOAD_SLOTS))
                        tile = adj_tiles[bass.ds(i * BODY + h // 2, 1), :, (h % 2) * HALF:(h % 2 + 1) * HALF]
                        nc.sync.dma_start(adj_sb[:, h % LOAD_SLOTS, :], tile.rearrange("o p c -> (o p) c")
                                          ).then_inc(loaded[h % LOAD_SLOTS], 16)
                bodies(sp, body)

                for g in range(GROUPS):
                    sp.wait_ge(out_stored[g], 16 * BODIES)

                sp.wait_ge(n_bad_ready, 1)
                n = sp.value_load(n_bad[0:1, 0:1], min_val=0, max_val=N)
                with sp.If(n > 0):
                    with sp.Fori(0, n) as r:
                        hold(sp, row_picked, r + 1, sp_spare)
                        row = sp.value_load(this_row[0:1, 0:1], min_val=0, max_val=N - 1)
                        nc.sync.dma_start(adj_row[:], adj[bass.ds(row, 1), :].rearrange(
                            "o (c q) -> (o c) q", q=P)).then_inc(row_loaded, 16)
                        nc.sync.dma_start(x_row[:], x[bass.ds(row, 1), :]).then_inc(row_loaded, 16)
                        hold(sp, row_done, r + 1, sp_spare)
                        nc.sync.dma_start(out[bass.ds(row, 1), :], r_out[:]).then_inc(row_stored, 16)
                        hold(sp, row_stored, (r + 1) * 16, sp_spare)

            @block.gpsimd
            def _(pool):
                nc.gpsimd.iota(offset[:], pattern=[[1, P]], base=0, channel_multiplier=-1).then_inc(iotas_ready, 1)
                nc.gpsimd.iota(code_base[:].rearrange("p t h s b -> p (t h) s b"),
                               pattern=[[0, PAIR], [-HALF, 2], [0, 8], [-FOLD, BITS]], base=N,
                               channel_multiplier=0).then_inc(iotas_ready, 1)
                nc.gpsimd.iota(row_id[:], pattern=[[P, TILES]], base=1, channel_multiplier=1).then_inc(iotas_ready, 1)
                nc.gpsimd.iota(edge_iota[:], pattern=[[1, EDGES]], base=0, channel_multiplier=0).then_inc(iotas_ready, 1)
                nc.gpsimd.iota(edge_id[:].rearrange("p (t c) -> p t c", c=CHUNKS), pattern=[[0, PAIR], [P, CHUNKS]],
                               base=0, channel_multiplier=1).then_inc(iotas_ready, 1)
                nc.gpsimd.iota(row_iota[:], pattern=[[1, P]], base=1, channel_multiplier=0).then_inc(iotas_ready, 1)
                nc.gpsimd.iota(slot_iota[:], pattern=[[1, SLOTS]], base=0, channel_multiplier=0).then_inc(iotas_ready, 1)

                pool.wait_ge(consts_ready, 1)

                def edges_to_rows(j, g):
                    hold(pool, edge_in_ready, count(j, g), pool_spare)
                    for c in range(PC):
                        last = nc.gpsimd.tensor_scalar(edge_row[:, g, c, :], row_iota[:],
                                                       edge_in[:, c, ROW_COL:ROW_COL + 1], None, ALU.is_equal)
                    last.then_inc(edge_row_made, 1)

                def spread_weights(j, g):
                    hold(pool, edge_w_ready, count(j, g), pool_spare)
                    nc.gpsimd.tensor_tensor(spread[:], edge_row[:, g, :, :],
                                            edge_w[:].unsqueeze(2).to_broadcast([P, PC, P]),
                                            ALU.mult).then_inc(spread_ready, 1)

                def norm_factors(j, g):
                    hold(pool, stats_ready, count(j, g), pool_spare)
                    if not (first(j) and g == 0):
                        hold(pool, scaled, count(j, g) - 1, pool_spare)
                    pool.sem_clear(p_step)
                    v = Steps(pool, p_step)
                    v.after(nc.gpsimd.tensor_tensor(var_eps[:], mean_var[:, :, 1], eps_all[:], ALU.add))
                    v.after(nc.gpsimd.tensor_tensor(rstd[:], var_eps[:], minus_half[:], ALU.pow))
                    v.after(nc.gpsimd.tensor_tensor(scaled_mean[:], mean_var[:, :, 0], rstd[:], ALU.mult))
                    nc.gpsimd.tensor_tensor(shift[:], scaled_mean[:], minus_one[:], ALU.mult
                                            ).then_inc(norm_ready, 1)

                def gather(j, g):
                        hold(pool, indexed, count(j, g), pool_spare)
                        if not first(j):
                            hold(pool, summed, count(j, g) - GROUPS, pool_spare)
                        for c in range(PC):
                            nc.gpsimd.indirect_dma_start(
                                out=nb[:, g, c, :], out_offset=None, in_=x[:, :],
                                in_offset=bass.IndirectOffsetOnAxis(ap=index[:, g, c:c + 1], axis=0),
                                bounds_check=N - 1, oob_is_err=False).then_inc(gathered[g], 16)

                def body(i):
                    for g in range(GROUPS):
                        p1, p2, p3 = (stage(i, g, k) for k in (1, 2, 3))
                        if p1:
                            edges_to_rows(*p1)
                            gather(*p1)
                        if p3:
                            norm_factors(*p3)
                        if p2:
                            spread_weights(*p2)
                bodies(pool, body)

            @block.scalar
            def _(act):
                act.wait_ge(w_turned, 1)
                nc.scalar.copy(WT_sb[:], misc[:, 0:P]).then_inc(wt_ready, 1)

                def square_half(i, g, q):
                    h = g * 2 * PAIR + q
                    act.wait_ge(loaded[h % LOAD_SLOTS], i * (16 * HALVES // LOAD_SLOTS)
                                + 16 * (h // LOAD_SLOTS + 1))
                    if not (first(i) and h < SQUARES):
                        act.wait_ge(folded, i * HALVES + (h + 1 - SQUARES))
                    if first(i) and h == SQUARES - 1:
                        act.wait_ge(s_ready, 1)
                    if q == 0 and not first(i):
                        act.wait_ge(listed, count(i, g) - GROUPS)
                    nc.scalar.activation(square[:, h % SQUARES, :], adj_sb[:, h % LOAD_SLOTS, :], ACT.Square,
                                         accum_out=half_sum[:, h:h + 1]).then_inc(squared, 1)

                def exp_weights(j, g):
                    act.wait_ge(scored, count(j, g))
                    nc.scalar.activation(weight[:], score_e[:], ACT.Exp).then_inc(weighed, 1)

                def exp_elu(j, g):
                    act.wait_ge(h_made, count(j, g))
                    nc.scalar.activation(z_exp[:], h_ps[:, :, 0:D], ACT.Exp).then_inc(elu_exp, 1)

                def distances(j, g):
                    act.wait_ge(middle_ready, count(j, g))
                    for t in range(PAIR):
                        last = nc.scalar.activation(from_middle[:, t, :], edge_iota[:], ACT.Abs,
                                                    bias=middle[:, t:t + 1])
                    last.then_inc(from_middle_made, 1)

                def copy_sums(j, g):
                    act.wait_ge(summed, count(j, g))
                    nc.scalar.copy(x_att[:], x_att_ps[:, :, 0:P]).then_inc(x_att_ready, 1)

                def scale(j, g):
                    act.wait_ge(norm_ready, count(j, g))
                    if not first(j):
                        act.wait_ge(out_stored[g], j * 16)
                    for t in range(PAIR):
                        last = nc.scalar.activation(y_out[:, g, t, :], y[:, t, :], ACT.Identity,
                                                    bias=shift[:, t:t + 1], scale=rstd[:, t:t + 1])
                    last.then_inc(scaled, 1)

                def store(j, g):
                    act.wait_ge(scaled, count(j, g))
                    nc.scalar.dma_start(out_tiles[:, bass.ds(j * BODY + g * PAIR, PAIR), :],
                                        y_out[:, g, :, :]).then_inc(out_stored[g], 16)

                def body(i):
                    for g in range(GROUPS):
                        now, p1, p2, p3, p4 = (stage(i, g, k) for k in range(5))
                        if now:
                            square_half(*now, 0)
                        if p4:
                            scale(*p4)
                            store(*p4)
                        if now:
                            square_half(*now, 1)
                        if p1:
                            distances(*p1)
                        if p3:
                            copy_sums(*p3)
                        if now:
                            square_half(*now, 2)
                        if p2:
                            exp_weights(*p2)
                        if p3:
                            exp_elu(*p3)
                        if now:
                            square_half(*now, 3)
                bodies(act, body)

                act.wait_ge(n_bad_ready, 1)
                n = act.value_load(n_bad[0:1, 0:1], min_val=0, max_val=N)
                with act.If(n > 0):
                    with act.Fori(0, n) as r:
                        hold(act, row_to_act, r * 2 + 1, act_spare)
                        nc.scalar.activation(r_w[:], r_e[:], ACT.Exp, bias=r_negmax_bc[:, 0:1],
                                             accum_out=r_wsum[:]).then_inc(act_to_row, 1)
                        hold(act, row_to_act, r * 2 + 2, act_spare)
                        nc.scalar.activation(r_zexp[:], r_zneg[:], ACT.Exp).then_inc(act_to_row, 1)

            @block.tensor
            def _(pe):
                pe.wait_ge(weights_loaded, 48)
                pe.wait_ge(consts_ready, 1)
                nc.tensor.transpose(misc[:, 0:P], W_sb[:], ident[:]).then_inc(w_turned, 1)
                pe.wait_ge(wt_ready, 1)
                for k in range(2):
                    last = nc.tensor.matmul(misc[:, P + k * D:P + (k + 1) * D], a_bc[:, k, :], WT_sb[:],
                                            start=True, stop=True)
                last.then_inc(wa_made, 1)
                for t in range(TILES):
                    if t % (TILES // 4) == 0:
                        pe.wait_ge(x_loaded[t // (TILES // 4)], 16)
                    last = nc.tensor.matmul(x_att_ps[:, 0, 0:1], x_sb[:, t, :], ones[:, 0:1],
                                            start=t == 0, stop=t == TILES - 1)
                last.then_inc(x_summed, 1)
                pe.wait_ge(x_mean_ready, 1)
                nc.tensor.transpose(misc[:, 0:P], x_mean_bc[:], ident[:]).then_inc(x_mean_turned, 1)

                def fold_half(i, g, q):
                    h = g * 2 * PAIR + q
                    pe.wait_ge(squared, i * HALVES + (h + 1))
                    if not (first(i) and h < LOAD_SLOTS):
                        pe.wait_ge(picked, i * HALVES + (h + 1 - LOAD_SLOTS))
                    for b in range(BITS):
                        last = nc.tensor.matmul(fold[:, h % LOAD_SLOTS, :], bit_ident[:, b, :],
                                                square[:, h % SQUARES, b * FOLD:(b + 1) * FOLD],
                                                start=b == 0, stop=b == BITS - 1)
                    last.then_inc(folded, 1)

                def chunk_of(g, c):
                    return row_edge[:, g, c // CHUNKS, (c % CHUNKS) * P:(c % CHUNKS + 1) * P]

                def count_starts(j, g):
                    pe.wait_ge(listed, count(j, g))
                    nc.tensor.matmul(starts_ps, before[:], found[:], start=True, stop=True).then_inc(starts_made, 1)

                def fill_edges(j, g):
                    pe.wait_ge(routed, count(j, g))
                    for c in range(PC):
                        last = nc.tensor.matmul(edge_in_ps[:, c, :], chunk_of(g, c), sent[:, c // CHUNKS, :],
                                                start=True, stop=True)
                    last.then_inc(edges_filled, 1)

                def send_scores(j, g):
                    pe.wait_ge(edge_row_made, count(j, g))
                    pe.wait_ge(t_ready, count(j, g))
                    for t in range(PAIR):
                        for c in range(CHUNKS):
                            last = nc.tensor.matmul(t_row_ps[:, t, :], edge_row[:, g, t * CHUNKS + c, :],
                                                    t_slot[:, t * CHUNKS + c, :],
                                                    start=c == 0, stop=c == CHUNKS - 1)
                    last.then_inc(t_sent, 1)

                def send_shares(j, g):
                    pe.wait_ge(shared, count(j, g))
                    for c in range(PC):
                        last = nc.tensor.matmul(share_ps[:, c, :], chunk_of(g, c), share[:, c // CHUNKS, :],
                                                start=True, stop=True)
                    last.then_inc(share_sent, 1)

                def sum_neighbours(j, g):
                    pe.wait_ge(spread_ready, count(j, g))
                    for t in range(PAIR):
                        for c in range(CHUNKS):
                            nc.tensor.matmul(x_att_ps[:, t, 0:P], nb[:, g, t * CHUNKS + c, :],
                                             spread[:, t * CHUNKS + c, :], start=c == 0, stop=False)
                        last = nc.tensor.matmul(x_att_ps[:, t, 0:P], x_mean_bc[:], empty_diag[:, t, :],
                                                start=False, stop=True)
                    last.then_inc(summed, 1)

                def times_W(j, g):
                    pe.wait_ge(x_att_ready, count(j, g))
                    for t in range(PAIR):
                        last = nc.tensor.matmul(h_ps[:, t, 0:D], x_att[:, t, :], W_sb[:], start=True, stop=True)
                    last.then_inc(h_made, 1)

                def body(i):
                    for g in range(GROUPS):
                        now, p1, p2, p3 = (stage(i, g, k) for k in range(4))
                        if now:
                            fold_half(*now, 0)
                        if p1:
                            count_starts(*p1)
                        if p3:
                            sum_neighbours(*p3)
                        if now:
                            fold_half(*now, 1)
                        if p2:
                            send_scores(*p2)
                        if p3:
                            times_W(*p3)
                        if p1:
                            fill_edges(*p1)
                        if now:
                            fold_half(*now, 2)
                            fold_half(*now, 3)
                        if p2:
                            send_shares(*p2)
                bodies(pe, body)

                pe.wait_ge(bad_counted, 1)
                nc.tensor.matmul(misc[0:1, 0:1], n_bad_f[:], ones[:, 0:1], start=True, stop=True
                                 ).then_inc(bad_summed, 1)
                pe.wait_ge(n_bad_ready, 1)
                n = pe.value_load(n_bad[0:1, 0:1], min_val=0, max_val=N)
                with pe.If(n > 0):
                    with pe.Fori(0, n) as r:
                        hold(pe, row_to_pe, r * 6 + 1, pe_spare)
                        nc.tensor.transpose(misc[0:1, 0:P], key_max[:], ident[:]).then_inc(pe_to_row, 1)
                        hold(pe, row_picked, r + 1, pe_spare)
                        nc.tensor.matmul(misc[:, P:P + 1], ones[0:1, :], this_key[:], start=True, stop=True
                                         ).then_inc(pe_to_row, 1)
                        hold(pe, row_to_pe, r * 6 + 2, pe_spare)
                        nc.tensor.matmul(misc[:, P + 1:P + 2], ones[0:1, :], r_s[:], start=True, stop=True
                                         ).then_inc(pe_to_row, 1)
                        hold(pe, row_to_pe, r * 6 + 3, pe_spare)
                        nc.tensor.transpose(misc[:, 2 * P:2 * P + TILES], mask[:], ident[0:TILES, 0:TILES]
                                            ).then_inc(pe_to_row, 1)
                        hold(pe, row_to_pe, r * 6 + 4, pe_spare)
                        nc.tensor.transpose(misc[0:1, 0:P], r_max[:], ident[:]).then_inc(pe_to_row, 1)
                        hold(pe, row_to_pe, r * 6 + 5, pe_spare)
                        nc.tensor.matmul(misc[:, P:P + 1], ones[0:1, :], r_negmax[:], start=True, stop=True
                                         ).then_inc(pe_to_row, 1)
                        hold(pe, act_to_row, r * 2 + 1, pe_spare)
                        nc.tensor.matmul(misc[0:1, 0:1], r_wsum[:], ones[:, 0:1], start=True, stop=True)
                        for c in range(TILES):
                            last = nc.tensor.matmul(x_att_ps[:, 0, 0:1], x_sb[:, c, :], r_w[:, c:c + 1],
                                                    start=c == 0, stop=c == TILES - 1)
                        last.then_inc(pe_to_row, 1)
                        hold(pe, row_to_pe, r * 6 + 6, pe_spare)
                        nc.tensor.matmul(h_ps[0:1, 0, 0:D], r_x[:], W_sb[:], start=True, stop=True
                                         ).then_inc(pe_to_row, 1)
                        hold(pe, row_done, r + 1, pe_spare)

            @block.vector
            def _(dve):
                s = Steps(dve, v_const)
                nc.vector.memset(nb[:], 0.0)
                nc.vector.memset(ones[:], 1.0)
                nc.vector.memset(minus_half[:], -0.5)
                nc.vector.memset(minus_one[:], -1.0)
                nc.vector.memset(eps_all[:], EPS)
                for b in range(BITS):
                    nc.vector.memset(bit_mask[:, b:b + 1], 1 << b)
                dve.wait_ge(iotas_ready, 7)
                s.after(nc.vector.tensor_scalar(ident[:], offset[:], 0.0, None, ALU.is_equal))
                for b in range(BITS):
                    last = nc.vector.tensor_scalar(bit_ident[:, b, :], ident[:], float(1 << b), None, ALU.mult)
                s.after(last)
                dve.wait_ge(weights_loaded, 48)
                nc.vector.tensor_scalar(before[:], offset[:], 0.0, None, ALU.is_gt)
                nc.vector.tensor_copy(sent[:, :, ROW_COL], row_id[:, 0:1].to_broadcast([P, PAIR]))
                for k in range(2):
                    last = nc.vector.tensor_scalar(a_bc[:, k, :], ones[:], a_sb[:, k:k + 1], None, ALU.mult)
                last.then_inc(consts_ready, 1)
                dve.wait_ge(wa_made, 1)
                s.after(nc.vector.tensor_copy(wa_bc[:].rearrange("p k c -> p (k c)"), misc[:, P:3 * P]))
                product = square[:, SQUARES - 1, :].bitcast(fp32).rearrange("p (t c) -> p t c", c=D)
                quarter = HALF * 2 // 4 // D
                for q in range(TILES // quarter):
                    dve.wait_ge(x_loaded[q * quarter * 4 // TILES], 16)
                    s.after(nc.vector.tensor_tensor(product, x_sb[:, q * quarter:(q + 1) * quarter, :],
                                                    wa_bc[:, 1:2, :].to_broadcast([P, quarter, D]), ALU.mult))
                    s.after(nc.vector.reduce_sum(s_all[:, q * quarter:(q + 1) * quarter], product, AX.X))
                nc.vector.engine_nop().then_inc(s_ready, 1)
                dve.wait_ge(x_summed, 1)
                s.after(nc.vector.tensor_scalar(x_mean[:], x_att_ps[:, 0, 0:1], 1.0 / N, None, ALU.mult))
                nc.vector.tensor_scalar(x_mean_bc[:], ones[:], x_mean[:, 0:1], None, ALU.mult
                                        ).then_inc(x_mean_ready, 1)
                dve.wait_ge(x_mean_turned, 1)
                s.after(nc.vector.tensor_copy(x_mean_bc[:], misc[:, 0:P]))

                v = None

                def pick(i, g, q):
                    h = g * 2 * PAIR + q
                    hold(dve, folded, i * HALVES + (h + 1), dve_spare)
                    v.after(nc.vector.max(top_map[:, q, :], fold[:, h % LOAD_SLOTS, :]))
                    nc.vector.max_index(top_col[:, q, :], top_map[:, q, :], fold[:, h % LOAD_SLOTS, :]
                                        ).then_inc(picked, 1)

                def lists(j, g):
                    cols = [P, 2 * PAIR * 8, BITS]
                    split = lambda t: t.rearrange("p t (c b) -> p (t c) b", b=BITS)
                    dve.wait_ge(picked, j * HALVES + (g + 1) * 2 * PAIR)
                    v.after(nc.vector.tensor_copy(top_int[:], top_map[:]))
                    nc.vector.tensor_tensor(
                        split(bit_set[:]),
                        top_int[:].rearrange("p q s -> p (q s)").unsqueeze(2).to_broadcast(cols),
                        bit_mask[:].unsqueeze(1).to_broadcast(cols), ALU.bitwise_and)
                    v.after(nc.vector.tensor_tensor(
                        split(code_all[:]), code_base[:].rearrange("p t h s b -> p (t h s) b"),
                        top_col[:].rearrange("p q s -> p (q s)").unsqueeze(2).to_broadcast(cols),
                        ALU.subtract))
                    v.after(nc.vector.scalar_tensor_tensor(cand[:], bit_set[:], 0.0, code_all[:],
                                                           ALU.is_gt, ALU.mult))
                    for t in range(PAIR):
                        v.after(nc.vector.max(code[:, t, 0:8], cand[:, t, :]))
                        v.after(nc.vector.match_replace(cand_rest[:, t, :], code[:, t, 0:8],
                                                        cand[:, t, :], 0.0))
                        last = nc.vector.max(code[:, t, 8:16], cand_rest[:, t, :])
                    v.after(last)
                    nc.vector.tensor_scalar(cap[:, g, :, :], code[:, :, 0:SLOTS], 1e30, NEG,
                                            ALU.mult, ALU.add)
                    nc.vector.tensor_copy(sent[:, :, 0:SLOTS], code[:, :, 0:SLOTS])
                    nc.vector.tensor_tensor(
                        expected[:], half_sum[:, g * 2 * PAIR:(g + 1) * 2 * PAIR:2],
                        half_sum[:, g * 2 * PAIR + 1:(g + 1) * 2 * PAIR:2], ALU.add)
                    v.after(nc.vector.tensor_scalar(is_code[:], code[:, :, 0:SLOTS], 0.0, None, ALU.is_gt))
                    v.after(nc.vector.reduce_sum(found[:], is_code[:], AX.X))
                    nc.vector.tensor_scalar(to_middle[:], found[:], -0.5, 0.5, ALU.mult, ALU.add)
                    nc.vector.tensor_scalar(half_len[:], found[:], 0.5, None, ALU.mult).then_inc(listed, 1)

                def route(j, g):
                    dve.wait_ge(starts_made, count(j, g))
                    nc.vector.scalar_tensor_tensor(middle[:], starts_ps, -1.0, to_middle[:], ALU.mult, ALU.add
                                                   ).then_inc(middle_ready, 1)
                    nc.vector.tensor_copy(sent[:, :, START_COL], starts_ps)
                    nc.vector.tensor_tensor(short[:], found[:], expected[:], ALU.not_equal)
                    v.after(nc.vector.tensor_tensor(ends[:], starts_ps, found[:], ALU.add))
                    v.after(nc.vector.tensor_scalar(over[:], ends[:], float(EDGES), None, ALU.is_gt))
                    nc.vector.tensor_tensor(bad[:, bass.ds(j * BODY + g * PAIR, PAIR)], short[:],
                                            over[:], ALU.max)

                def rows_to_edges(j, g):
                    dve.wait_ge(from_middle_made, count(j, g))
                    for t in range(PAIR):
                        last = nc.vector.tensor_scalar(row_edge[:, g, t, :], from_middle[:, t, :],
                                                       half_len[:, t:t + 1], None, ALU.is_lt)
                    last.then_inc(routed, 1)

                def indices(j, g):
                    slots = [P, PC, SLOTS]
                    dve.wait_ge(edges_filled, count(j, g))
                    if not (first(j) and g == 0):
                        dve.wait_ge(edge_row_made, count(j, g) - 1)
                    nc.vector.tensor_copy(edge_in[:], edge_in_ps).then_inc(edge_in_ready, 1)
                    dve.wait_ge(edge_in_ready, count(j, g))
                    v.after(nc.vector.tensor_tensor(slot_of[:], edge_id[:], edge_in[:, :, START_COL],
                                                    ALU.subtract))
                    v.after(nc.vector.tensor_tensor(at_slot[:, g, :, :],
                                                    slot_iota[:].unsqueeze(1).to_broadcast(slots),
                                                    slot_of[:].unsqueeze(2).to_broadcast(slots),
                                                    ALU.is_equal))
                    v.after(nc.vector.tensor_tensor(own_code[:], edge_in[:, :, 0:SLOTS],
                                                    at_slot[:, g, :, :], ALU.mult))
                    v.after(nc.vector.reduce_sum(edge_code[:], own_code[:], AX.X))
                    if not first(j):
                        dve.wait_ge(gathered[g], j * (16 * PC))
                    nc.vector.tensor_scalar(index[:, g, :], edge_code[:], -1.0, float(N),
                                            ALU.mult, ALU.add).then_inc(indexed, 1)
                    nc.vector.tensor_scalar(empty[:, g, :], found[:], 0.0, None, ALU.is_equal)
                def neighbour_scores(j, g):
                    dve.wait_ge(gathered[g], (j + 1) * (16 * PC))
                    for c in range(PC):
                        last = nc.vector.tensor_tensor_reduce(
                            out=dot[:, c, :], in0=nb[:, g, c, :], in1=wa_bc[:, 0, :], scale=1.0, scalar=0.0,
                            op0=ALU.mult, op1=ALU.add, accum_out=t_edge[:, c:c + 1])
                    v.after(last)
                    nc.vector.tensor_tensor(t_slot[:], at_slot[:, g, :, :],
                                            t_edge[:].unsqueeze(2).to_broadcast([P, PC, SLOTS]),
                                            ALU.mult).then_inc(t_ready, 1)

                def scores(j, g):
                    slots = [P, PAIR, SLOTS]
                    dve.wait_ge(t_sent, count(j, g))
                    mine = s_all[:, bass.ds(j * BODY + g * PAIR, PAIR)]
                    v.after(nc.vector.tensor_tensor(score[:], t_row_ps, mine.unsqueeze(2).to_broadcast(slots),
                                                    ALU.add))
                    v.after(nc.vector.scalar_tensor_tensor(score_l[:], score[:], ALPHA, score[:],
                                                           ALU.mult, ALU.max))
                    v.after(nc.vector.tensor_tensor(score_l[:], score_l[:], cap[:, g, :, :], ALU.min))
                    v.after(nc.vector.reduce_max(row_max[:], score_l[:], AX.X))
                    nc.vector.tensor_tensor(score_e[:], score_l[:],
                                            row_max[:].unsqueeze(2).to_broadcast(slots),
                                            ALU.subtract).then_inc(scored, 1)

                def weights(j, g):
                    dve.wait_ge(weighed, count(j, g))
                    v.after(nc.vector.reduce_sum(w_sum[:], weight[:], AX.X))
                    v.after(nc.vector.reciprocal(w_inv[:], w_sum[:]))
                    nc.vector.tensor_tensor(share[:], weight[:],
                                            w_inv[:].unsqueeze(2).to_broadcast([P, PAIR, SLOTS]),
                                            ALU.mult).then_inc(shared, 1)

                def edge_weights(j, g):
                    dve.wait_ge(share_sent, count(j, g))
                    for t in range(PAIR):
                        nc.vector.tensor_scalar(empty_diag[:, t, :], ident[:], empty[:, g, t:t + 1], None, ALU.mult)
                    v.after(nc.vector.tensor_tensor(own_share[:], share_ps, at_slot[:, g, :, :], ALU.mult))
                    nc.vector.reduce_sum(edge_w[:], own_share[:], AX.X).then_inc(edge_w_ready, 1)

                def finish(j, g):
                    mine = bass.ds(j * BODY + g * PAIR, PAIR)
                    dve.wait_ge(elu_exp, count(j, g))
                    v.after(nc.vector.tensor_scalar(z_one[:], z_exp[:], 1.0, None, ALU.min))
                    v.after(nc.vector.scalar_tensor_tensor(elu[:], h_ps[:, :, 0:D], 1.0, z_one[:],
                                                           ALU.add, ALU.max))
                    if not (first(j) and g == 0):
                        dve.wait_ge(scaled, count(j, g) - 1)
                    v.after(nc.vector.scalar_tensor_tensor(y[:], elu[:], -1.0, x_sb[:, mine, :],
                                                           ALU.add, ALU.add))
                    for t in range(PAIR):
                        last = nc.vector.bn_stats(stats[:, t, :], y[:, t, :])
                    v.after(last)
                    for t in range(PAIR):
                        last = nc.vector.bn_aggr(mean_var[:, t, :], stats[:, t, :])
                    last.then_inc(stats_ready, 1)

                def body(i):
                    nonlocal v
                    for g in range(GROUPS):
                        now, p1, p2, p3 = (stage(i, g, k) for k in range(4))
                        dve.sem_clear(v_step)
                        v = Steps(dve, v_step)
                        if now:
                            pick(*now, 0)
                        if p1:
                            route(*p1)
                        if p2:
                            neighbour_scores(*p2)
                        if now:
                            pick(*now, 1)
                        if p1:
                            rows_to_edges(*p1)
                        if p2:
                            scores(*p2)
                        if p1:
                            indices(*p1)
                        if now:
                            pick(*now, 2)
                        if p2:
                            weights(*p2)
                        if p3:
                            finish(*p3)
                        if now:
                            pick(*now, 3)
                        if p2:
                            edge_weights(*p2)
                        if now:
                            lists(*now)

                def norm(v, y, parts, var, var_e, guess, inv, t1, t2):
                    for part, st, mv in parts:
                        last = nc.vector.bn_stats(st, part)
                    v.after(last)
                    for part, st, mv in parts:
                        last = nc.vector.bn_aggr(mv, st)
                    v.after(last)
                    v.after(nc.vector.tensor_scalar(var_e, var, EPS, None, ALU.add))
                    v.after(nc.vector.tensor_scalar(guess, var_e.bitcast(i32), 1, None, ALU.logical_shift_right))
                    v.after(nc.vector.tensor_scalar(inv.bitcast(i32), guess, -1.0, float(0x5f3759df),
                                                    ALU.mult, ALU.add))
                    for _ in range(3):
                        v.after(nc.vector.tensor_tensor(t1, inv, inv, ALU.mult))
                        v.after(nc.vector.scalar_tensor_tensor(t2, t1, -0.5, var_e, ALU.mult, ALU.mult))
                        v.after(nc.vector.scalar_tensor_tensor(inv, t2, 1.5, inv, ALU.add, ALU.mult))

                bodies(dve, body)

                dve.wait_ge(indexed, BODIES * GROUPS)
                nc.vector.tensor_tensor(key[:], bad[:], row_id[:], ALU.mult)
                nc.vector.reduce_sum(n_bad_f[:], bad[:], AX.X).then_inc(bad_counted, 1)
                dve.wait_ge(bad_summed, 1)
                nc.vector.tensor_copy(n_bad[:], misc[0:1, 0:1]).then_inc(n_bad_ready, 1)
                dve.wait_ge(n_bad_ready, 1)
                n = dve.value_load(n_bad[0:1, 0:1], min_val=0, max_val=N)
                with dve.If(n > 0):
                    product = adj_sb[:, 0:2, :].bitcast(fp32).rearrange("p s (t c) -> p (s t) c", c=D)
                    e = Steps(dve, v_rows)
                    e.after(nc.vector.tensor_tensor(product, x_sb[:], wa_bc[:, 0:1, :].to_broadcast([P, TILES, D]),
                                                    ALU.mult))
                    e.after(nc.vector.reduce_sum(t_all[:], product, AX.X))
                    with dve.Fori(0, n) as r:
                        dve.sem_clear(v_row)
                        v = Steps(dve, v_row)
                        nc.vector.reduce_max(key_max[:], key[:], AX.X).then_inc(row_to_pe, 1)
                        hold(dve, pe_to_row, r * 8 + 1, dve_spare)
                        v.after(nc.vector.reduce_max(this_key[:], misc[0:1, 0:P], AX.X))
                        nc.vector.tensor_scalar(this_row[:], this_key[:], -1.0, None, ALU.add).then_inc(row_picked, 1)
                        hold(dve, pe_to_row, r * 8 + 2, dve_spare)
                        v.after(nc.vector.tensor_copy(key_bc[:], misc[:, P:P + 1]))
                        v.after(nc.vector.scalar_tensor_tensor(key[:], key[:], key_bc[:, 0:1], key[:],
                                                               ALU.is_lt, ALU.mult))
                        hold(dve, row_loaded, (r + 1) * 32, dve_spare)
                        v.after(nc.vector.tensor_tensor(x_dot[:], x_row[:], wa_bc[0:1, 1, :], ALU.mult))
                        nc.vector.reduce_sum(r_s[:], x_dot[:], AX.X).then_inc(row_to_pe, 1)
                        nc.vector.tensor_scalar(mask[:], adj_row[:], 0.0, None, ALU.is_gt).then_inc(row_to_pe, 1)
                        hold(dve, pe_to_row, r * 8 + 3, dve_spare)
                        v.after(nc.vector.tensor_copy(s_bc[:], misc[:, P + 1:P + 2]))
                        v.after(nc.vector.tensor_scalar(r_score[:], t_all[:], s_bc[:, 0:1], None, ALU.add))
                        nc.vector.scalar_tensor_tensor(r_lrelu[:], r_score[:], ALPHA, r_score[:], ALU.mult, ALU.max)
                        hold(dve, pe_to_row, r * 8 + 4, dve_spare)
                        v.after(nc.vector.tensor_copy(maskT[:], misc[:, 2 * P:2 * P + TILES]))
                        nc.vector.tensor_scalar(r_neg[:], maskT[:], -NEG, NEG, ALU.mult, ALU.add)
                        v.after(nc.vector.tensor_tensor(r_e[:], r_lrelu[:], maskT[:], ALU.mult))
                        v.after(nc.vector.tensor_tensor(r_e[:], r_e[:], r_neg[:], ALU.add))
                        nc.vector.reduce_max(r_max[:], r_e[:], AX.X).then_inc(row_to_pe, 1)
                        hold(dve, pe_to_row, r * 8 + 5, dve_spare)
                        nc.vector.tensor_reduce(r_negmax[:], misc[0:1, 0:P], AX.X, ALU.max, negate=True
                                                ).then_inc(row_to_pe, 1)
                        hold(dve, pe_to_row, r * 8 + 6, dve_spare)
                        nc.vector.tensor_copy(r_negmax_bc[:], misc[:, P:P + 1]).then_inc(row_to_act, 1)
                        hold(dve, pe_to_row, r * 8 + 7, dve_spare)
                        nc.vector.tensor_copy(r_x[:], x_att_ps[:, 0, 0:1]).then_inc(row_to_pe, 1)
                        v.after(nc.vector.reciprocal(r_inv[:], misc[0:1, 0:1]))
                        hold(dve, pe_to_row, r * 8 + 8, dve_spare)
                        v.after(nc.vector.tensor_scalar(r_z[:], h_ps[0:1, 0, 0:D], r_inv[:, 0:1], None, ALU.mult))
                        nc.vector.tensor_scalar(r_zneg[:], r_z[:], 0.0, None, ALU.min).then_inc(row_to_act, 1)
                        hold(dve, act_to_row, r * 2 + 2, dve_spare)
                        v.after(nc.vector.scalar_tensor_tensor(r_elu[:], r_z[:], 0.0, r_zexp[:], ALU.max, ALU.add))
                        v.after(nc.vector.scalar_tensor_tensor(r_y[:], r_elu[:], -1.0, x_row[:], ALU.add, ALU.add))
                        norm(v, r_y, [(r_y[:], stats[0:1, 0, :], mean_var[0:1, 0, :])], mean_var[0:1, 0, 1:2],
                             var_eps[0:1, 0:1], guess_i[0:1, 0:1], rstd[0:1, 0:1], newton[0:1, 0:1],
                             newton2[0:1, 0:1])
                        nc.vector.tensor_scalar(r_out[:], r_y[:], mean_var[0:1, 0, 0:1], rstd[0:1, 0:1],
                                                ALU.subtract, ALU.mult).then_inc(row_done, 1)
                        hold(dve, row_stored, (r + 1) * 16, dve_spare)


_INS = ['x', 'adj', 'L0_gnn_W', 'L0_gnn_a']
_OUTS = [((8192, 128), 'float32')]


def kernel(**inputs):
    import numpy as _np
    import concourse.bacc as _bacc
    from concourse import mybir as _mybir
    from concourse.bass_utils import run_bass_kernel_spmd as _run

    nc = _bacc.Bacc("TRN2", target_bir_lowering=False, num_devices=1)
    arrays, args = {}, []
    for name in _INS:
        a = _np.ascontiguousarray(inputs[name])
        arrays[f"in_{name}"] = a
        args.append(nc.dram_tensor(f"in_{name}", a.shape, _mybir.dt.from_np(a.dtype), kind="ExternalInput").ap())
    for i, (shape, dtype) in enumerate(_OUTS):
        dt = _mybir.dt.from_np(_np.dtype(dtype))
        args.append(nc.dram_tensor(f"out_{i}", shape, dt, kind="ExternalOutput").ap())
    graph_attention(nc, *args)
    r = _run(nc, [arrays], core_ids=[0])
    return r.results[0]["out_0"]
```

```python
from contextlib import ExitStack

import concourse.bass as bass
from concourse import mybir

SLOTS = 10
CHUNKS = 5
NEG = -9000000000000000.0
ALPHA = 0.2
EPS = 1e-5


class Steps:

    def __init__(self, eng, sem):
        self.eng, self.sem, self.n = eng, sem, 0

    def after(self, instruction):
        self.n += 1
        instruction.then_inc(self.sem, 1)
        self.eng.wait_ge(self.sem, self.n)


def hold(eng, sem, value, spare):
    eng.wait_ge(sem, value)
    eng.sem_inc(spare, 1)


def graph_attention(nc, x, adj, W, a, out):
    fp32, i32, u32, bf16 = mybir.dt.float32, mybir.dt.int32, mybir.dt.uint32, mybir.dt.bfloat16
    ACT, ALU, AX = mybir.ActivationFunctionType, mybir.AluOpType, mybir.AxisListType

    N, D = x.shape
    P = 128
    assert D == P and adj.shape[0] == N and adj.shape[1] == N
    TILES = N // P
    HALF = N // 2
    BITS = 8
    FOLD = HALF // BITS
    assert FOLD == 512
    PAIR = 2
    GROUPS = 2
    BODY = PAIR * GROUPS
    BODIES = TILES // BODY
    HALVES = 2 * BODY
    LOAD_SLOTS = 4
    SQUARES = 4
    CAND = 2 * 8 * BITS
    EDGES = CHUNKS * P // PAIR

    def pieces(t):
        for c in range(CHUNKS):
            lo, hi = max(c * P, t * EDGES), min((c + 1) * P, (t + 1) * EDGES)
            if lo < hi:
                yield c, lo - c * P, hi - c * P, lo - t * EDGES

    SPANS = [[piece[0] for piece in pieces(t)] for t in range(PAIR)]
    SPAN = len(SPANS[0])
    assert all(len(span) == SPAN for span in SPANS)
    ROW_COL, START_COL = SLOTS, SLOTS + 1
    SENT = SLOTS + 2

    adj_tiles = adj.rearrange("(t p) c -> t p c", p=P)
    out_tiles = out.rearrange("(t p) c -> p t c", p=P)
    x_tiles = x.rearrange("(t p) c -> p t c", p=P)

    with ExitStack() as stack:
        sb = lambda name, shape, dt: stack.enter_context(nc.sbuf_tensor(name, shape, dt))
        ps = lambda name, shape, dt: stack.enter_context(nc.psum_tensor(name, shape, dt))
        sem = lambda name: stack.enter_context(nc.semaphore(name))

        x_sb = sb("x_sb", [P, TILES, D], fp32)
        adj_sb = sb("adj_sb", [P, LOAD_SLOTS, HALF], i32)
        square = sb("square", [P, SQUARES, HALF], bf16)
        ident = sb("ident", [P, P], fp32)
        bit_ident = sb("bit_ident", [P, BITS, P], bf16)
        bit_mask = sb("bit_mask", [P, BITS], i32)
        code_base = sb("code_base", [P, PAIR, 2, 8, BITS], i32)
        row_id = sb("row_id", [P, TILES], i32)
        offset = sb("offset", [P, P], i32)
        before = sb("before", [P, P], fp32)
        edge_iota = sb("edge_iota", [P, EDGES], i32)
        edge_id = sb("edge_id", [P, CHUNKS], i32)
        tile_edge = sb("tile_edge", [P, PAIR], fp32)
        row_iota = sb("row_iota", [P, PAIR * P], i32)
        slot_iota = sb("slot_iota", [P, SLOTS], i32)
        ones = sb("ones", [P, P], fp32)
        W_sb = sb("W_sb", [P, D], fp32)
        WT_sb = sb("WT_sb", [P, D], fp32)
        a_sb = sb("a_sb", [P, 2], fp32)
        a_bc = sb("a_bc", [P, 2, P], fp32)
        wa_bc = sb("wa_bc", [P, 2, D], fp32)
        x_mean = sb("x_mean", [P, 1], fp32)
        x_mean_bc = sb("x_mean_bc", [P, P], fp32)
        s_all = sb("s_all", [P, TILES], fp32)
        eps_all = sb("eps_all", [P, PAIR], fp32)
        minus_half = sb("minus_half", [P, PAIR], fp32)
        minus_one = sb("minus_one", [P, PAIR], fp32)

        half_sum = sb("half_sum", [P, HALVES], fp32)
        top_map = sb("top_map", [P, 2 * PAIR, 8], fp32)
        top_col = sb("top_col", [P, 2 * PAIR, 8], u32)
        top_int = sb("top_int", [P, 2 * PAIR, 8], i32)
        bit_set = sb("bit_set", [P, PAIR, CAND], i32)
        code_all = sb("code_all", [P, PAIR, CAND], fp32)
        cand = sb("cand", [P, PAIR, CAND], fp32)
        cand_rest = sb("cand_rest", [P, PAIR, CAND], fp32)
        code = sb("code", [P, PAIR, 16], fp32)
        is_code = sb("is_code", [P, PAIR, SLOTS], fp32)
        found = sb("found", [P, PAIR], fp32)
        expected = sb("expected", [P, PAIR], fp32)
        short = sb("short", [P, PAIR], fp32)
        ends = sb("ends", [P, PAIR], fp32)
        half_len = sb("half_len", [P, PAIR], fp32)
        to_middle = sb("to_middle", [P, PAIR], fp32)
        middle = sb("middle", [P, PAIR], fp32)
        from_middle = sb("from_middle", [P, PAIR, EDGES], fp32)
        over = sb("over", [P, PAIR], fp32)
        bad = sb("bad", [P, TILES], fp32)
        cap = sb("cap", [P, GROUPS, PAIR, SLOTS], fp32)
        empty = sb("empty", [P, GROUPS, PAIR], fp32)
        sent = sb("sent", [P, PAIR, SENT], fp32)
        row_edge = sb("row_edge", [P, GROUPS, PAIR, EDGES], fp32)
        edge_in = sb("edge_in", [P, CHUNKS, SENT], fp32)
        slot_of = sb("slot_of", [P, CHUNKS], fp32)
        at_slot = sb("at_slot", [P, GROUPS, CHUNKS, SLOTS], fp32)
        own_code = sb("own_code", [P, CHUNKS, SLOTS], fp32)
        edge_code = sb("edge_code", [P, CHUNKS], fp32)
        index = sb("index", [P, GROUPS, CHUNKS], u32)
        edge_row = sb("edge_row", [P, GROUPS, PAIR, SPAN, P], fp32)

        nb = sb("nb", [P, GROUPS + 1, CHUNKS, D], fp32)
        dot = sb("dot", [P, CHUNKS, D], fp32)
        t_edge = sb("t_edge", [P, CHUNKS], fp32)
        t_slot = sb("t_slot", [P, CHUNKS, SLOTS], fp32)
        score = sb("score", [P, PAIR, SLOTS], fp32)
        score_l = sb("score_l", [P, PAIR, SLOTS], fp32)
        score_e = sb("score_e", [P, PAIR, SLOTS], fp32)
        weight = sb("weight", [P, PAIR, SLOTS], fp32)
        share = sb("share", [P, PAIR, SLOTS], fp32)
        row_max = sb("row_max", [P, PAIR], fp32)
        w_sum = sb("w_sum", [P, PAIR], fp32)
        w_inv = sb("w_inv", [P, PAIR], fp32)
        own_share = sb("own_share", [P, CHUNKS, SLOTS], fp32)
        edge_w = sb("edge_w", [P, CHUNKS], fp32)
        spread = sb("spread", [P, PAIR, SPAN, P], fp32)
        x_att = sb("x_att", [P, PAIR, P], fp32)
        empty_diag = sb("empty_diag", [P, PAIR, P], fp32)
        z_one = sb("z_one", [P, PAIR, D], fp32)
        z_exp = sb("z_exp", [P, PAIR, D], fp32)
        elu = sb("elu", [P, PAIR, D], fp32)
        y = sb("y", [P, PAIR, D], fp32)
        stats = sb("stats", [P, PAIR, 6], fp32)
        mean_var = sb("mean_var", [P, PAIR, 2], fp32)
        var_eps = sb("var_eps", [P, PAIR], fp32)
        guess_i = sb("guess_i", [P, PAIR], i32)
        rstd = sb("rstd", [P, PAIR], fp32)
        scaled_mean = sb("scaled_mean", [P, PAIR], fp32)
        shift = sb("shift", [P, PAIR], fp32)
        newton = sb("newton", [P, PAIR], fp32)
        newton2 = sb("newton2", [P, PAIR], fp32)
        y_out = sb("y_out", [P, GROUPS, PAIR, D], fp32)

        n_bad_f = sb("n_bad_f", [P, 1], fp32)
        n_bad = sb("n_bad", [1, 1], i32)
        key = sb("key", [P, TILES], fp32)
        key_max = sb("key_max", [P, 1], fp32)
        this_key = sb("this_key", [1, 1], fp32)
        this_row = sb("this_row", [1, 1], i32)
        key_bc = sb("key_bc", [P, 1], fp32)
        adj_row = sb("adj_row", [TILES, P], i32)
        x_row = sb("x_row", [1, D], fp32)
        t_all = sb("t_all", [P, TILES], fp32)
        x_dot = sb("x_dot", [1, D], fp32)
        r_s = sb("r_s", [1, 1], fp32)
        s_bc = sb("s_bc", [P, 1], fp32)
        r_x = sb("r_x", [P, 1], fp32)
        mask = sb("mask", [TILES, P], fp32)
        maskT = sb("maskT", [P, TILES], fp32)
        r_score = sb("r_score", [P, TILES], fp32)
        r_lrelu = sb("r_lrelu", [P, TILES], fp32)
        r_neg = sb("r_neg", [P, TILES], fp32)
        r_e = sb("r_e", [P, TILES], fp32)
        r_max = sb("r_max", [P, 1], fp32)
        r_negmax = sb("r_negmax", [1, 1], fp32)
        r_negmax_bc = sb("r_negmax_bc", [P, 1], fp32)
        r_w = sb("r_w", [P, TILES], fp32)
        r_wsum = sb("r_wsum", [P, 1], fp32)
        r_inv = sb("r_inv", [1, 1], fp32)
        r_z = sb("r_z", [1, D], fp32)
        r_zneg = sb("r_zneg", [1, D], fp32)
        r_zexp = sb("r_zexp", [1, D], fp32)
        r_elu = sb("r_elu", [1, D], fp32)
        r_y = sb("r_y", [1, D], fp32)
        r_out = sb("r_out", [1, D], fp32)

        fold = ps("fold", [P, LOAD_SLOTS, FOLD], fp32)
        small = ps("small", [P, 512], fp32)
        x_att_ps = ps("x_att_ps", [P, PAIR, 256], fp32)
        h_ps = ps("h_ps", [P, PAIR, 256], fp32)
        misc = ps("misc", [P, 512], fp32)
        starts_ps = misc[:, 160:160 + PAIR]
        edge_in_ps = small[:, 64:64 + CHUNKS * SENT].rearrange("p (c k) -> p c k", k=SENT)
        t_row_ps = misc[:, 192:192 + PAIR * SLOTS].rearrange("p (t k) -> p t k", k=SLOTS)
        share_ps = small[:, 256:256 + CHUNKS * SLOTS].rearrange("p (c k) -> p c k", k=SLOTS)

        x_loaded = [sem(f"x_loaded{q}") for q in range(4)]
        weights_loaded = sem("weights_loaded")
        loaded = [sem(f"loaded{s}") for s in range(LOAD_SLOTS)]
        gathered = [sem(f"gathered{g}") for g in range(GROUPS)]
        out_stored = [sem(f"out_stored{g}") for g in range(GROUPS)]
        iotas_ready = sem("iotas_ready")
        v_const = sem("v_const")
        consts_ready = sem("consts_ready")
        w_turned = sem("w_turned")
        wt_ready = sem("wt_ready")
        wa_made = sem("wa_made")
        x_summed = sem("x_summed")
        x_mean_ready = sem("x_mean_ready")
        x_mean_turned = sem("x_mean_turned")
        squared = sem("squared")
        folded = sem("folded")
        picked = sem("picked")
        listed = sem("listed")
        v_step = sem("v_step")
        starts_made = sem("starts_made")
        routed = sem("routed")
        edges_filled = sem("edges_filled")
        indexed = sem("indexed")
        edge_in_ready = sem("edge_in_ready")
        edge_row_made = sem("edge_row_made")
        edge_w_ready = sem("edge_w_ready")
        stats_ready = sem("stats_ready")
        p_step = sem("p_step")
        norm_ready = sem("norm_ready")
        scaled = sem("scaled")
        s_ready = sem("s_ready")
        middle_ready = sem("middle_ready")
        from_middle_made = sem("from_middle_made")
        t_ready = sem("t_ready")
        t_sent = sem("t_sent")
        scored = sem("scored")
        weighed = sem("weighed")
        shared = sem("shared")
        share_sent = sem("share_sent")
        spread_ready = sem("spread_ready")
        summed = sem("summed")
        x_att_ready = sem("x_att_ready")
        h_made = sem("h_made")
        elu_exp = sem("elu_exp")
        bad_counted = sem("bad_counted")
        bad_summed = sem("bad_summed")
        n_bad_ready = sem("n_bad_ready")
        v_rows = sem("v_rows")
        v_row = sem("v_row")
        row_to_pe = sem("row_to_pe")
        pe_to_row = sem("pe_to_row")
        row_picked = sem("row_picked")
        row_loaded = sem("row_loaded")
        row_to_act = sem("row_to_act")
        act_to_row = sem("act_to_row")
        row_done = sem("row_done")
        row_stored = sem("row_stored")
        sp_spare, pool_spare, act_spare, pe_spare, dve_spare = [
            sem(f"{e}_spare") for e in ("sp", "pool", "act", "pe", "dve")]

        def stage(i, g, k):
            j, place = i - (k - g + 1) // GROUPS, (g - k) % GROUPS
            return None if isinstance(j, int) and not 0 <= j < BODIES else (j, place)

        def steps(eng, step):
            for n in range(3 * GROUPS):
                step(n // GROUPS, n % GROUPS)
            with eng.Fori(3, BODIES - 1) as i:
                for g in range(GROUPS):
                    step(i, g)
            for g in range(GROUPS - 1):
                step(BODIES - 1, g)

        final = (BODIES - 1, GROUPS - 1)
        back1, back2, back3, back4 = (stage(*final, k) for k in range(1, 5))
        is_final = lambda j, g: isinstance(j, int) and (j, g) == final
        nb_of = lambda j, g: nb[:, GROUPS if is_final(j, g) else g, :, :]

        first = lambda j: isinstance(j, int) and j == 0
        count = lambda j, g: j * GROUPS + (g + 1)

        def edges_to_rows(eng, j, g):
            for t in range(PAIR):
                for k, c in enumerate(SPANS[t]):
                    last_one = eng.tensor_scalar(edge_row[:, g, t, k, :], row_iota[:, t * P:(t + 1) * P],
                                                 edge_in[:, c, ROW_COL:ROW_COL + 1], None, ALU.is_equal)
            last_one.then_inc(edge_row_made, 1)

        with nc.Block() as block:

            @block.sync
            def _(sp):
                nc.sync.dma_start(W_sb[:], W).then_inc(weights_loaded, 16)
                with nc.allow_non_contiguous_dma(reason="256 numbers, one per partition"):
                    nc.sync.dma_start(a_sb[:, 0:1], a[D:2 * D, :]).then_inc(weights_loaded, 16)
                    nc.sync.dma_start(a_sb[:, 1:2], a[0:D, :]).then_inc(weights_loaded, 16)
                Q = TILES // 4
                for q in range(4):
                    nc.sync.dma_start(x_sb[:, q * Q:(q + 1) * Q, :],
                                      x_tiles[:, q * Q:(q + 1) * Q, :]).then_inc(x_loaded[q], 16)

                def step(i, g):
                    for h in range(g * 2 * PAIR, (g + 1) * 2 * PAIR):
                        if not (first(i) and h < LOAD_SLOTS):
                            sp.wait_ge(squared, i * HALVES + (h + 1 - LOAD_SLOTS))
                        tile = adj_tiles[bass.ds(i * BODY + h // 2, 1), :, (h % 2) * HALF:(h % 2 + 1) * HALF]
                        nc.sync.dma_start(adj_sb[:, h % LOAD_SLOTS, :], tile.rearrange("o p c -> (o p) c")
                                          ).then_inc(loaded[h % LOAD_SLOTS], 16)
                steps(sp, step)
                step(*final)

                for g in range(GROUPS):
                    sp.wait_ge(out_stored[g], 16 * BODIES)

                sp.wait_ge(n_bad_ready, 1)
                n = sp.value_load(n_bad[0:1, 0:1], min_val=0, max_val=N)
                with sp.If(n > 0):
                    with sp.Fori(0, n) as r:
                        hold(sp, row_picked, r + 1, sp_spare)
                        row = sp.value_load(this_row[0:1, 0:1], min_val=0, max_val=N - 1)
                        nc.sync.dma_start(adj_row[:], adj[bass.ds(row, 1), :].rearrange(
                            "o (c q) -> (o c) q", q=P)).then_inc(row_loaded, 16)
                        nc.sync.dma_start(x_row[:], x[bass.ds(row, 1), :]).then_inc(row_loaded, 16)
                        hold(sp, row_done, r + 1, sp_spare)
                        nc.sync.dma_start(out[bass.ds(row, 1), :], r_out[:]).then_inc(row_stored, 16)
                        hold(sp, row_stored, (r + 1) * 16, sp_spare)

            @block.gpsimd
            def _(pool):
                nc.gpsimd.iota(offset[:], pattern=[[1, P]], base=0, channel_multiplier=-1).then_inc(iotas_ready, 1)
                nc.gpsimd.iota(code_base[:].rearrange("p t h s b -> p (t h) s b"),
                               pattern=[[0, PAIR], [-HALF, 2], [0, 8], [-FOLD, BITS]], base=N,
                               channel_multiplier=0).then_inc(iotas_ready, 1)
                nc.gpsimd.iota(row_id[:], pattern=[[P, TILES]], base=1, channel_multiplier=1).then_inc(iotas_ready, 1)
                nc.gpsimd.iota(edge_iota[:], pattern=[[1, EDGES]], base=0, channel_multiplier=0).then_inc(iotas_ready, 1)
                nc.gpsimd.iota(edge_id[:], pattern=[[P, CHUNKS]], base=0, channel_multiplier=1).then_inc(iotas_ready, 1)
                nc.gpsimd.iota(row_iota[:], pattern=[[1, PAIR * P]], base=1, channel_multiplier=0).then_inc(iotas_ready, 1)
                nc.gpsimd.iota(slot_iota[:], pattern=[[1, SLOTS]], base=0, channel_multiplier=0).then_inc(iotas_ready, 1)

                pool.wait_ge(consts_ready, 1)

                def spread_weights(j, g):
                    hold(pool, edge_w_ready, count(j, g), pool_spare)
                    for t in range(PAIR):
                        mine = edge_w[:, SPANS[t][0]:SPANS[t][0] + SPAN]
                        last = nc.gpsimd.tensor_tensor(spread[:, t, :, :], edge_row[:, g, t, :, :],
                                                       mine.unsqueeze(2).to_broadcast([P, SPAN, P]), ALU.mult)
                    last.then_inc(spread_ready, 1)

                def norm_factors(j, g):
                    hold(pool, stats_ready, count(j, g), pool_spare)
                    if not (first(j) and g == 0):
                        hold(pool, scaled, count(j, g) - 1, pool_spare)
                    pool.sem_clear(p_step)
                    v = Steps(pool, p_step)
                    v.after(nc.gpsimd.tensor_tensor(var_eps[:], mean_var[:, :, 1], eps_all[:], ALU.add))
                    v.after(nc.gpsimd.tensor_tensor(rstd[:], var_eps[:], minus_half[:], ALU.pow))
                    v.after(nc.gpsimd.tensor_tensor(scaled_mean[:], mean_var[:, :, 0], rstd[:], ALU.mult))
                    nc.gpsimd.tensor_tensor(shift[:], scaled_mean[:], minus_one[:], ALU.mult
                                            ).then_inc(norm_ready, 1)

                def gather(j, g):
                    hold(pool, indexed, count(j, g), pool_spare)
                    if not first(j) and not is_final(j, g):
                        hold(pool, summed, count(j, g) - GROUPS, pool_spare)
                    for c in range(CHUNKS):
                        nc.gpsimd.indirect_dma_start(
                            out=nb_of(j, g)[:, c, :], out_offset=None, in_=x[:, :],
                            in_offset=bass.IndirectOffsetOnAxis(ap=index[:, g, c:c + 1], axis=0),
                            bounds_check=N - 1, oob_is_err=False).then_inc(gathered[g], 16)

                def step(i, g):
                    p1, p2, p3 = (stage(i, g, k) for k in (1, 2, 3))
                    if p1:
                        hold(pool, edge_in_ready, count(*p1), pool_spare)
                        edges_to_rows(nc.gpsimd, *p1)
                        gather(*p1)
                    if p3:
                        norm_factors(*p3)
                    if p2:
                        spread_weights(*p2)

                steps(pool, step)

                gather(*back1)
                spread_weights(*back2)
                gather(*final)
                norm_factors(*back3)
                spread_weights(*back1)
                norm_factors(*back2)
                spread_weights(*final)
                norm_factors(*back1)
                norm_factors(*final)

            @block.scalar
            def _(act):
                act.wait_ge(w_turned, 1)
                nc.scalar.copy(WT_sb[:], misc[:, 0:P]).then_inc(wt_ready, 1)

                def square_half(i, g, q):
                    h = g * 2 * PAIR + q
                    act.wait_ge(loaded[h % LOAD_SLOTS], i * (16 * HALVES // LOAD_SLOTS)
                                + 16 * (h // LOAD_SLOTS + 1))
                    if not (first(i) and h < SQUARES):
                        act.wait_ge(folded, i * HALVES + (h + 1 - SQUARES))
                    if first(i) and h == SQUARES - 1:
                        act.wait_ge(s_ready, 1)
                    if q == 0 and not first(i):
                        act.wait_ge(listed, count(i, g) - GROUPS)
                    nc.scalar.activation(square[:, h % SQUARES, :], adj_sb[:, h % LOAD_SLOTS, :], ACT.Square,
                                         accum_out=half_sum[:, h:h + 1]).then_inc(squared, 1)

                def exp_weights(j, g):
                    act.wait_ge(scored, count(j, g))
                    nc.scalar.activation(weight[:], score_e[:], ACT.Exp).then_inc(weighed, 1)

                def exp_elu(j, g):
                    act.wait_ge(h_made, count(j, g))
                    nc.scalar.activation(z_exp[:], h_ps[:, :, 0:D], ACT.Exp).then_inc(elu_exp, 1)

                def distances(j, g):
                    act.wait_ge(middle_ready, count(j, g))
                    for t in range(PAIR):
                        last = nc.scalar.activation(from_middle[:, t, :], edge_iota[:], ACT.Abs,
                                                    bias=middle[:, t:t + 1])
                    last.then_inc(from_middle_made, 1)

                def copy_sums(j, g):
                    act.wait_ge(summed, count(j, g))
                    nc.scalar.copy(x_att[:], x_att_ps[:, :, 0:P]).then_inc(x_att_ready, 1)

                def scale(j, g):
                    act.wait_ge(norm_ready, count(j, g))
                    if not first(j):
                        act.wait_ge(out_stored[g], j * 16)
                    for t in range(PAIR):
                        last = nc.scalar.activation(y_out[:, g, t, :], y[:, t, :], ACT.Identity,
                                                    bias=shift[:, t:t + 1], scale=rstd[:, t:t + 1])
                    last.then_inc(scaled, 1)

                def store(j, g):
                    act.wait_ge(scaled, count(j, g))
                    nc.scalar.dma_start(out_tiles[:, bass.ds(j * BODY + g * PAIR, PAIR), :],
                                        y_out[:, g, :, :]).then_inc(out_stored[g], 16)

                def step(i, g):
                    now, p1, p2, p3, p4 = (stage(i, g, k) for k in range(5))
                    square_half(*now, 0)
                    if p4:
                        scale(*p4)
                        store(*p4)
                    square_half(*now, 1)
                    if p1:
                        distances(*p1)
                    if p3:
                        copy_sums(*p3)
                    square_half(*now, 2)
                    if p2:
                        exp_weights(*p2)
                    if p3:
                        exp_elu(*p3)
                    square_half(*now, 3)

                steps(act, step)

                for q in range(2 * PAIR):
                    square_half(*final, q)
                distances(*back1)
                scale(*back4)
                store(*back4)
                exp_weights(*back2)
                copy_sums(*back3)
                distances(*final)
                exp_weights(*back1)
                exp_elu(*back3)
                copy_sums(*back2)
                scale(*back3)
                store(*back3)
                exp_elu(*back2)
                copy_sums(*back1)
                exp_weights(*final)
                scale(*back2)
                store(*back2)
                exp_elu(*back1)
                copy_sums(*final)
                scale(*back1)
                store(*back1)
                exp_elu(*final)
                scale(*final)
                store(*final)

                act.wait_ge(n_bad_ready, 1)
                n = act.value_load(n_bad[0:1, 0:1], min_val=0, max_val=N)
                with act.If(n > 0):
                    with act.Fori(0, n) as r:
                        hold(act, row_to_act, r * 2 + 1, act_spare)
                        nc.scalar.activation(r_w[:], r_e[:], ACT.Exp, bias=r_negmax_bc[:, 0:1],
                                             accum_out=r_wsum[:]).then_inc(act_to_row, 1)
                        hold(act, row_to_act, r * 2 + 2, act_spare)
                        nc.scalar.activation(r_zexp[:], r_zneg[:], ACT.Exp).then_inc(act_to_row, 1)

            @block.tensor
            def _(pe):
                pe.wait_ge(weights_loaded, 48)
                pe.wait_ge(consts_ready, 1)
                nc.tensor.transpose(misc[:, 0:P], W_sb[:], ident[:]).then_inc(w_turned, 1)
                pe.wait_ge(wt_ready, 1)
                for k in range(2):
                    last = nc.tensor.matmul(misc[:, P + k * D:P + (k + 1) * D], a_bc[:, k, :], WT_sb[:],
                                            start=True, stop=True)
                last.then_inc(wa_made, 1)
                for t in range(TILES):
                    if t % (TILES // 4) == 0:
                        pe.wait_ge(x_loaded[t // (TILES // 4)], 16)
                    last = nc.tensor.matmul(x_att_ps[:, 0, 0:1], x_sb[:, t, :], ones[:, 0:1],
                                            start=t == 0, stop=t == TILES - 1)
                last.then_inc(x_summed, 1)
                pe.wait_ge(x_mean_ready, 1)
                nc.tensor.transpose(misc[:, 0:P], x_mean_bc[:], ident[:]).then_inc(x_mean_turned, 1)

                def fold_half(i, g, q):
                    h = g * 2 * PAIR + q
                    pe.wait_ge(squared, i * HALVES + (h + 1))
                    if not (first(i) and h < LOAD_SLOTS):
                        pe.wait_ge(picked, i * HALVES + (h + 1 - LOAD_SLOTS))
                    for b in range(BITS):
                        last = nc.tensor.matmul(fold[:, h % LOAD_SLOTS, :], bit_ident[:, b, :],
                                                square[:, h % SQUARES, b * FOLD:(b + 1) * FOLD],
                                                start=b == 0, stop=b == BITS - 1)
                    last.then_inc(folded, 1)

                def count_starts(j, g):
                    pe.wait_ge(listed, count(j, g))
                    nc.tensor.matmul(starts_ps, before[:], found[:], start=True, stop=True).then_inc(starts_made, 1)

                def fill_edges(j, g):
                    pe.wait_ge(routed, count(j, g))
                    for t in range(PAIR):
                        for c, lo, hi, e in pieces(t):
                            last = nc.tensor.matmul(edge_in_ps[lo:hi, c, :], row_edge[:, g, t, e:e + hi - lo],
                                                    sent[:, t, :], start=True, stop=True)
                    last.then_inc(edges_filled, 1)

                def send_scores(j, g):
                    pe.wait_ge(edge_row_made, count(j, g))
                    pe.wait_ge(t_ready, count(j, g))
                    for t in range(PAIR):
                        for k, c in enumerate(SPANS[t]):
                            last = nc.tensor.matmul(t_row_ps[:, t, :], edge_row[:, g, t, k, :], t_slot[:, c, :],
                                                    start=k == 0, stop=k == SPAN - 1)
                    last.then_inc(t_sent, 1)

                def send_shares(j, g):
                    pe.wait_ge(shared, count(j, g))
                    for t in range(PAIR):
                        for c, lo, hi, e in pieces(t):
                            last = nc.tensor.matmul(share_ps[lo:hi, c, :], row_edge[:, g, t, e:e + hi - lo],
                                                    share[:, t, :], start=True, stop=True)
                    last.then_inc(share_sent, 1)

                def sum_neighbours(j, g):
                    pe.wait_ge(spread_ready, count(j, g))
                    for t in range(PAIR):
                        for k, c in enumerate(SPANS[t]):
                            nc.tensor.matmul(x_att_ps[:, t, 0:P], nb_of(j, g)[:, c, :], spread[:, t, k, :],
                                             start=k == 0, stop=False)
                        last = nc.tensor.matmul(x_att_ps[:, t, 0:P], x_mean_bc[:], empty_diag[:, t, :],
                                                start=False, stop=True)
                    last.then_inc(summed, 1)

                def times_W(j, g):
                    pe.wait_ge(x_att_ready, count(j, g))
                    for t in range(PAIR):
                        last = nc.tensor.matmul(h_ps[:, t, 0:D], x_att[:, t, :], W_sb[:], start=True, stop=True)
                    last.then_inc(h_made, 1)

                def step(i, g):
                    now, p1, p2, p3 = (stage(i, g, k) for k in range(4))
                    fold_half(*now, 0)
                    if p1:
                        count_starts(*p1)
                    if p3:
                        sum_neighbours(*p3)
                    fold_half(*now, 1)
                    if p2:
                        send_scores(*p2)
                    if p3:
                        times_W(*p3)
                    if p1:
                        fill_edges(*p1)
                    fold_half(*now, 2)
                    fold_half(*now, 3)
                    if p2:
                        send_shares(*p2)

                def keep_warm(products):
                    for _ in range(products):
                        nc.tensor.matmul(fold[:, 0, :], bit_ident[:, 0, :], square[:, 0, 0:FOLD],
                                         start=True, stop=True)

                steps(pe, step)

                fold_half(*final, 0)
                fold_half(*final, 1)
                count_starts(*back1)
                fold_half(*final, 2)
                fold_half(*final, 3)
                fill_edges(*back1)
                send_scores(*back2)
                sum_neighbours(*back3)
                send_shares(*back2)
                keep_warm(7)
                count_starts(*final)
                keep_warm(7)
                fill_edges(*final)
                send_scores(*back1)
                times_W(*back3)
                sum_neighbours(*back2)
                send_shares(*back1)
                pe.wait_ge(stats_ready, count(*back3))
                times_W(*back2)
                keep_warm(3)
                send_scores(*final)
                sum_neighbours(*back1)
                send_shares(*final)
                times_W(*back1)
                keep_warm(4)
                sum_neighbours(*final)
                pe.wait_ge(stats_ready, count(*back1))
                times_W(*final)

                pe.wait_ge(bad_counted, 1)
                nc.tensor.matmul(misc[0:1, 0:1], n_bad_f[:], ones[:, 0:1], start=True, stop=True
                                 ).then_inc(bad_summed, 1)
                pe.wait_ge(n_bad_ready, 1)
                n = pe.value_load(n_bad[0:1, 0:1], min_val=0, max_val=N)
                with pe.If(n > 0):
                    with pe.Fori(0, n) as r:
                        hold(pe, row_to_pe, r * 6 + 1, pe_spare)
                        nc.tensor.transpose(misc[0:1, 0:P], key_max[:], ident[:]).then_inc(pe_to_row, 1)
                        hold(pe, row_picked, r + 1, pe_spare)
                        nc.tensor.matmul(misc[:, P:P + 1], ones[0:1, :], this_key[:], start=True, stop=True
                                         ).then_inc(pe_to_row, 1)
                        hold(pe, row_to_pe, r * 6 + 2, pe_spare)
                        nc.tensor.matmul(misc[:, P + 1:P + 2], ones[0:1, :], r_s[:], start=True, stop=True
                                         ).then_inc(pe_to_row, 1)
                        hold(pe, row_to_pe, r * 6 + 3, pe_spare)
                        nc.tensor.transpose(misc[:, 2 * P:2 * P + TILES], mask[:], ident[0:TILES, 0:TILES]
                                            ).then_inc(pe_to_row, 1)
                        hold(pe, row_to_pe, r * 6 + 4, pe_spare)
                        nc.tensor.transpose(misc[0:1, 0:P], r_max[:], ident[:]).then_inc(pe_to_row, 1)
                        hold(pe, row_to_pe, r * 6 + 5, pe_spare)
                        nc.tensor.matmul(misc[:, P:P + 1], ones[0:1, :], r_negmax[:], start=True, stop=True
                                         ).then_inc(pe_to_row, 1)
                        hold(pe, act_to_row, r * 2 + 1, pe_spare)
                        nc.tensor.matmul(misc[0:1, 0:1], r_wsum[:], ones[:, 0:1], start=True, stop=True)
                        for c in range(TILES):
                            last = nc.tensor.matmul(x_att_ps[:, 0, 0:1], x_sb[:, c, :], r_w[:, c:c + 1],
                                                    start=c == 0, stop=c == TILES - 1)
                        last.then_inc(pe_to_row, 1)
                        hold(pe, row_to_pe, r * 6 + 6, pe_spare)
                        nc.tensor.matmul(h_ps[0:1, 0, 0:D], r_x[:], W_sb[:], start=True, stop=True
                                         ).then_inc(pe_to_row, 1)
                        hold(pe, row_done, r + 1, pe_spare)

            @block.vector
            def _(dve):
                s = Steps(dve, v_const)
                nc.vector.memset(nb[:], 0.0)
                nc.vector.memset(ones[:], 1.0)
                nc.vector.memset(minus_half[:], -0.5)
                nc.vector.memset(minus_one[:], -1.0)
                nc.vector.memset(eps_all[:], EPS)
                for b in range(BITS):
                    nc.vector.memset(bit_mask[:, b:b + 1], 1 << b)
                for t in range(PAIR):
                    nc.vector.memset(tile_edge[:, t:t + 1], float(t * EDGES))
                dve.wait_ge(iotas_ready, 7)
                s.after(nc.vector.tensor_scalar(ident[:], offset[:], 0.0, None, ALU.is_equal))
                for b in range(BITS):
                    last = nc.vector.tensor_scalar(bit_ident[:, b, :], ident[:], float(1 << b), None, ALU.mult)
                s.after(last)
                dve.wait_ge(weights_loaded, 48)
                nc.vector.tensor_scalar(before[:], offset[:], 0.0, None, ALU.is_gt)
                nc.vector.tensor_copy(sent[:, :, ROW_COL], row_id[:, 0:PAIR])
                for k in range(2):
                    last = nc.vector.tensor_scalar(a_bc[:, k, :], ones[:], a_sb[:, k:k + 1], None, ALU.mult)
                last.then_inc(consts_ready, 1)
                dve.wait_ge(wa_made, 1)
                s.after(nc.vector.tensor_copy(wa_bc[:].rearrange("p k c -> p (k c)"), misc[:, P:3 * P]))
                product = square[:, SQUARES - 1, :].bitcast(fp32).rearrange("p (t c) -> p t c", c=D)
                quarter = HALF * 2 // 4 // D
                for q in range(TILES // quarter):
                    dve.wait_ge(x_loaded[q * quarter * 4 // TILES], 16)
                    s.after(nc.vector.tensor_tensor(product, x_sb[:, q * quarter:(q + 1) * quarter, :],
                                                    wa_bc[:, 1:2, :].to_broadcast([P, quarter, D]), ALU.mult))
                    s.after(nc.vector.reduce_sum(s_all[:, q * quarter:(q + 1) * quarter], product, AX.X))
                nc.vector.engine_nop().then_inc(s_ready, 1)
                dve.wait_ge(x_summed, 1)
                s.after(nc.vector.tensor_scalar(x_mean[:], x_att_ps[:, 0, 0:1], 1.0 / N, None, ALU.mult))
                nc.vector.tensor_scalar(x_mean_bc[:], ones[:], x_mean[:, 0:1], None, ALU.mult
                                        ).then_inc(x_mean_ready, 1)
                dve.wait_ge(x_mean_turned, 1)
                s.after(nc.vector.tensor_copy(x_mean_bc[:], misc[:, 0:P]))

                v = None

                def pick(i, g, q):
                    h = g * 2 * PAIR + q
                    hold(dve, folded, i * HALVES + (h + 1), dve_spare)
                    v.after(nc.vector.max(top_map[:, q, :], fold[:, h % LOAD_SLOTS, :]))
                    nc.vector.max_index(top_col[:, q, :], top_map[:, q, :], fold[:, h % LOAD_SLOTS, :]
                                        ).then_inc(picked, 1)

                def lists(j, g):
                    cols = [P, 2 * PAIR * 8, BITS]
                    split = lambda t: t.rearrange("p t (c b) -> p (t c) b", b=BITS)
                    dve.wait_ge(picked, j * HALVES + (g + 1) * 2 * PAIR)
                    v.after(nc.vector.tensor_copy(top_int[:], top_map[:]))
                    nc.vector.tensor_tensor(
                        split(bit_set[:]),
                        top_int[:].rearrange("p q s -> p (q s)").unsqueeze(2).to_broadcast(cols),
                        bit_mask[:].unsqueeze(1).to_broadcast(cols), ALU.bitwise_and)
                    v.after(nc.vector.tensor_tensor(
                        split(code_all[:]), code_base[:].rearrange("p t h s b -> p (t h s) b"),
                        top_col[:].rearrange("p q s -> p (q s)").unsqueeze(2).to_broadcast(cols),
                        ALU.subtract))
                    v.after(nc.vector.scalar_tensor_tensor(cand[:], bit_set[:], 0.0, code_all[:],
                                                           ALU.is_gt, ALU.mult))
                    for t in range(PAIR):
                        v.after(nc.vector.max(code[:, t, 0:8], cand[:, t, :]))
                        v.after(nc.vector.match_replace(cand_rest[:, t, :], code[:, t, 0:8],
                                                        cand[:, t, :], 0.0))
                        last = nc.vector.max(code[:, t, 8:16], cand_rest[:, t, :])
                    v.after(last)
                    nc.vector.tensor_scalar(cap[:, g, :, :], code[:, :, 0:SLOTS], 1e30, NEG,
                                            ALU.mult, ALU.add)
                    nc.vector.tensor_copy(sent[:, :, 0:SLOTS], code[:, :, 0:SLOTS])
                    nc.vector.tensor_tensor(
                        expected[:], half_sum[:, g * 2 * PAIR:(g + 1) * 2 * PAIR:2],
                        half_sum[:, g * 2 * PAIR + 1:(g + 1) * 2 * PAIR:2], ALU.add)
                    v.after(nc.vector.tensor_scalar(is_code[:], code[:, :, 0:SLOTS], 0.0, None, ALU.is_gt))
                    v.after(nc.vector.reduce_sum(found[:], is_code[:], AX.X))
                    nc.vector.tensor_scalar(to_middle[:], found[:], -0.5, 0.5, ALU.mult, ALU.add)
                    nc.vector.tensor_scalar(half_len[:], found[:], 0.5, None, ALU.mult).then_inc(listed, 1)

                def route(j, g):
                    dve.wait_ge(starts_made, count(j, g))
                    nc.vector.scalar_tensor_tensor(middle[:], starts_ps, -1.0, to_middle[:], ALU.mult, ALU.add
                                                   ).then_inc(middle_ready, 1)
                    nc.vector.tensor_tensor(sent[:, :, START_COL], starts_ps, tile_edge[:], ALU.add)
                    nc.vector.tensor_tensor(short[:], found[:], expected[:], ALU.not_equal)
                    v.after(nc.vector.tensor_tensor(ends[:], starts_ps, found[:], ALU.add))
                    v.after(nc.vector.tensor_scalar(over[:], ends[:], float(EDGES), None, ALU.is_gt))
                    nc.vector.tensor_tensor(bad[:, bass.ds(j * BODY + g * PAIR, PAIR)], short[:],
                                            over[:], ALU.max)

                def rows_to_edges(j, g):
                    dve.wait_ge(from_middle_made, count(j, g))
                    for t in range(PAIR):
                        last = nc.vector.tensor_scalar(row_edge[:, g, t, :], from_middle[:, t, :],
                                                       half_len[:, t:t + 1], None, ALU.is_lt)
                    last.then_inc(routed, 1)

                def indices(j, g):
                    slots = [P, CHUNKS, SLOTS]
                    dve.wait_ge(edges_filled, count(j, g))
                    if not (first(j) and g == 0):
                        dve.wait_ge(edge_row_made, count(j, g) - 1)
                    nc.vector.tensor_copy(edge_in[:], edge_in_ps).then_inc(edge_in_ready, 1)
                    dve.wait_ge(edge_in_ready, count(j, g))
                    v.after(nc.vector.tensor_tensor(slot_of[:], edge_id[:], edge_in[:, :, START_COL],
                                                    ALU.subtract))
                    v.after(nc.vector.tensor_tensor(at_slot[:, g, :, :],
                                                    slot_iota[:].unsqueeze(1).to_broadcast(slots),
                                                    slot_of[:].unsqueeze(2).to_broadcast(slots),
                                                    ALU.is_equal))
                    v.after(nc.vector.tensor_tensor(own_code[:], edge_in[:, :, 0:SLOTS],
                                                    at_slot[:, g, :, :], ALU.mult))
                    v.after(nc.vector.reduce_sum(edge_code[:], own_code[:], AX.X))
                    if not first(j):
                        dve.wait_ge(gathered[g], j * (16 * CHUNKS))
                    nc.vector.tensor_scalar(index[:, g, :], edge_code[:], -1.0, float(N),
                                            ALU.mult, ALU.add).then_inc(indexed, 1)
                    nc.vector.tensor_scalar(empty[:, g, :], found[:], 0.0, None, ALU.is_equal)

                def neighbour_scores(j, g):
                    dve.wait_ge(gathered[g], (j + 1) * (16 * CHUNKS))
                    for c in range(CHUNKS):
                        last = nc.vector.tensor_tensor_reduce(
                            out=dot[:, c, :], in0=nb_of(j, g)[:, c, :], in1=wa_bc[:, 0, :], scale=1.0, scalar=0.0,
                            op0=ALU.mult, op1=ALU.add, accum_out=t_edge[:, c:c + 1])
                    v.after(last)
                    nc.vector.tensor_tensor(t_slot[:], at_slot[:, g, :, :],
                                            t_edge[:].unsqueeze(2).to_broadcast([P, CHUNKS, SLOTS]),
                                            ALU.mult).then_inc(t_ready, 1)

                def scores(j, g):
                    slots = [P, PAIR, SLOTS]
                    dve.wait_ge(t_sent, count(j, g))
                    mine = s_all[:, bass.ds(j * BODY + g * PAIR, PAIR)]
                    v.after(nc.vector.tensor_tensor(score[:], t_row_ps, mine.unsqueeze(2).to_broadcast(slots),
                                                    ALU.add))
                    v.after(nc.vector.scalar_tensor_tensor(score_l[:], score[:], ALPHA, score[:],
                                                           ALU.mult, ALU.max))
                    v.after(nc.vector.tensor_tensor(score_l[:], score_l[:], cap[:, g, :, :], ALU.min))
                    v.after(nc.vector.reduce_max(row_max[:], score_l[:], AX.X))
                    nc.vector.tensor_tensor(score_e[:], score_l[:],
                                            row_max[:].unsqueeze(2).to_broadcast(slots),
                                            ALU.subtract).then_inc(scored, 1)

                def weights(j, g):
                    dve.wait_ge(weighed, count(j, g))
                    v.after(nc.vector.reduce_sum(w_sum[:], weight[:], AX.X))
                    v.after(nc.vector.reciprocal(w_inv[:], w_sum[:]))
                    nc.vector.tensor_tensor(share[:], weight[:],
                                            w_inv[:].unsqueeze(2).to_broadcast([P, PAIR, SLOTS]),
                                            ALU.mult).then_inc(shared, 1)

                def edge_weights(j, g):
                    dve.wait_ge(share_sent, count(j, g))
                    for t in range(PAIR):
                        nc.vector.tensor_scalar(empty_diag[:, t, :], ident[:], empty[:, g, t:t + 1], None, ALU.mult)
                    v.after(nc.vector.tensor_tensor(own_share[:], share_ps, at_slot[:, g, :, :], ALU.mult))
                    nc.vector.reduce_sum(edge_w[:], own_share[:], AX.X).then_inc(edge_w_ready, 1)

                def finish(j, g):
                    mine = bass.ds(j * BODY + g * PAIR, PAIR)
                    dve.wait_ge(elu_exp, count(j, g))
                    v.after(nc.vector.tensor_scalar(z_one[:], z_exp[:], 1.0, None, ALU.min))
                    v.after(nc.vector.scalar_tensor_tensor(elu[:], h_ps[:, :, 0:D], 1.0, z_one[:],
                                                           ALU.add, ALU.max))
                    if not (first(j) and g == 0):
                        dve.wait_ge(scaled, count(j, g) - 1)
                    v.after(nc.vector.scalar_tensor_tensor(y[:], elu[:], -1.0, x_sb[:, mine, :],
                                                           ALU.add, ALU.add))
                    for t in range(PAIR):
                        last = nc.vector.bn_stats(stats[:, t, :], y[:, t, :])
                    v.after(last)
                    for t in range(PAIR):
                        last = nc.vector.bn_aggr(mean_var[:, t, :], stats[:, t, :])
                    last.then_inc(stats_ready, 1)

                def fresh_steps():
                    nonlocal v
                    dve.sem_clear(v_step)
                    v = Steps(dve, v_step)

                def step(i, g):
                    now, p1, p2, p3 = (stage(i, g, k) for k in range(4))
                    fresh_steps()
                    pick(*now, 0)
                    if p1:
                        route(*p1)
                    if p2:
                        neighbour_scores(*p2)
                    pick(*now, 1)
                    if p1:
                        rows_to_edges(*p1)
                    if p2:
                        scores(*p2)
                    if p1:
                        indices(*p1)
                    pick(*now, 2)
                    if p2:
                        weights(*p2)
                    if p3:
                        finish(*p3)
                    pick(*now, 3)
                    if p2:
                        edge_weights(*p2)
                    lists(*now)

                def norm(v, y, parts, var, var_e, guess, inv, t1, t2):
                    for part, st, mv in parts:
                        last = nc.vector.bn_stats(st, part)
                    v.after(last)
                    for part, st, mv in parts:
                        last = nc.vector.bn_aggr(mv, st)
                    v.after(last)
                    v.after(nc.vector.tensor_scalar(var_e, var, EPS, None, ALU.add))
                    v.after(nc.vector.tensor_scalar(guess, var_e.bitcast(i32), 1, None, ALU.logical_shift_right))
                    v.after(nc.vector.tensor_scalar(inv.bitcast(i32), guess, -1.0, float(0x5f3759df),
                                                    ALU.mult, ALU.add))
                    for _ in range(3):
                        v.after(nc.vector.tensor_tensor(t1, inv, inv, ALU.mult))
                        v.after(nc.vector.scalar_tensor_tensor(t2, t1, -0.5, var_e, ALU.mult, ALU.mult))
                        v.after(nc.vector.scalar_tensor_tensor(inv, t2, 1.5, inv, ALU.add, ALU.mult))

                steps(dve, step)

                fresh_steps()
                pick(*final, 0)
                route(*back1)
                pick(*final, 1)
                pick(*final, 2)
                rows_to_edges(*back1)
                neighbour_scores(*back2)
                pick(*final, 3)
                indices(*back1)
                scores(*back2)
                weights(*back2)
                lists(*final)
                route(*final)
                edge_weights(*back2)
                rows_to_edges(*final)
                dve.wait_ge(spread_ready, count(*back3))
                edges_to_rows(nc.vector, *back1)
                neighbour_scores(*back1)
                indices(*final)
                dve.wait_ge(spread_ready, count(*back2))
                edges_to_rows(nc.vector, *final)
                scores(*back1)
                weights(*back1)
                finish(*back3)
                edge_weights(*back1)
                neighbour_scores(*final)
                finish(*back2)
                scores(*final)
                weights(*final)
                edge_weights(*final)
                finish(*back1)
                finish(*final)

                dve.wait_ge(indexed, BODIES * GROUPS)
                nc.vector.tensor_tensor(key[:], bad[:], row_id[:], ALU.mult)
                nc.vector.reduce_sum(n_bad_f[:], bad[:], AX.X).then_inc(bad_counted, 1)
                dve.wait_ge(bad_summed, 1)
                nc.vector.tensor_copy(n_bad[:], misc[0:1, 0:1]).then_inc(n_bad_ready, 1)
                dve.wait_ge(n_bad_ready, 1)
                n = dve.value_load(n_bad[0:1, 0:1], min_val=0, max_val=N)
                with dve.If(n > 0):
                    product = adj_sb[:, 0:2, :].bitcast(fp32).rearrange("p s (t c) -> p (s t) c", c=D)
                    e = Steps(dve, v_rows)
                    e.after(nc.vector.tensor_tensor(product, x_sb[:], wa_bc[:, 0:1, :].to_broadcast([P, TILES, D]),
                                                    ALU.mult))
                    e.after(nc.vector.reduce_sum(t_all[:], product, AX.X))
                    with dve.Fori(0, n) as r:
                        dve.sem_clear(v_row)
                        v = Steps(dve, v_row)
                        nc.vector.reduce_max(key_max[:], key[:], AX.X).then_inc(row_to_pe, 1)
                        hold(dve, pe_to_row, r * 8 + 1, dve_spare)
                        v.after(nc.vector.reduce_max(this_key[:], misc[0:1, 0:P], AX.X))
                        nc.vector.tensor_scalar(this_row[:], this_key[:], -1.0, None, ALU.add).then_inc(row_picked, 1)
                        hold(dve, pe_to_row, r * 8 + 2, dve_spare)
                        v.after(nc.vector.tensor_copy(key_bc[:], misc[:, P:P + 1]))
                        v.after(nc.vector.scalar_tensor_tensor(key[:], key[:], key_bc[:, 0:1], key[:],
                                                               ALU.is_lt, ALU.mult))
                        hold(dve, row_loaded, (r + 1) * 32, dve_spare)
                        v.after(nc.vector.tensor_tensor(x_dot[:], x_row[:], wa_bc[0:1, 1, :], ALU.mult))
                        nc.vector.reduce_sum(r_s[:], x_dot[:], AX.X).then_inc(row_to_pe, 1)
                        hold(dve, pe_to_row, r * 8 + 3, dve_spare)
                        v.after(nc.vector.tensor_copy(s_bc[:], misc[:, P + 1:P + 2]))
                        nc.vector.tensor_scalar(mask[:], adj_row[:], 0.0, None, ALU.is_gt).then_inc(row_to_pe, 1)
                        v.after(nc.vector.tensor_scalar(r_score[:], t_all[:], s_bc[:, 0:1], None, ALU.add))
                        nc.vector.scalar_tensor_tensor(r_lrelu[:], r_score[:], ALPHA, r_score[:], ALU.mult, ALU.max)
                        hold(dve, pe_to_row, r * 8 + 4, dve_spare)
                        v.after(nc.vector.tensor_copy(maskT[:], misc[:, 2 * P:2 * P + TILES]))
                        nc.vector.tensor_scalar(r_neg[:], maskT[:], -NEG, NEG, ALU.mult, ALU.add)
                        v.after(nc.vector.tensor_tensor(r_e[:], r_lrelu[:], maskT[:], ALU.mult))
                        v.after(nc.vector.tensor_tensor(r_e[:], r_e[:], r_neg[:], ALU.add))
                        nc.vector.reduce_max(r_max[:], r_e[:], AX.X).then_inc(row_to_pe, 1)
                        hold(dve, pe_to_row, r * 8 + 5, dve_spare)
                        nc.vector.tensor_reduce(r_negmax[:], misc[0:1, 0:P], AX.X, ALU.max, negate=True
                                                ).then_inc(row_to_pe, 1)
                        hold(dve, pe_to_row, r * 8 + 6, dve_spare)
                        nc.vector.tensor_copy(r_negmax_bc[:], misc[:, P:P + 1]).then_inc(row_to_act, 1)
                        hold(dve, pe_to_row, r * 8 + 7, dve_spare)
                        nc.vector.tensor_copy(r_x[:], x_att_ps[:, 0, 0:1]).then_inc(row_to_pe, 1)
                        v.after(nc.vector.reciprocal(r_inv[:], misc[0:1, 0:1]))
                        hold(dve, pe_to_row, r * 8 + 8, dve_spare)
                        v.after(nc.vector.tensor_scalar(r_z[:], h_ps[0:1, 0, 0:D], r_inv[:, 0:1], None, ALU.mult))
                        nc.vector.tensor_scalar(r_zneg[:], r_z[:], 0.0, None, ALU.min).then_inc(row_to_act, 1)
                        hold(dve, act_to_row, r * 2 + 2, dve_spare)
                        v.after(nc.vector.scalar_tensor_tensor(r_elu[:], r_z[:], 0.0, r_zexp[:], ALU.max, ALU.add))
                        v.after(nc.vector.scalar_tensor_tensor(r_y[:], r_elu[:], -1.0, x_row[:], ALU.add, ALU.add))
                        norm(v, r_y, [(r_y[:], stats[0:1, 0, :], mean_var[0:1, 0, :])], mean_var[0:1, 0, 1:2],
                             var_eps[0:1, 0:1], guess_i[0:1, 0:1], rstd[0:1, 0:1], newton[0:1, 0:1],
                             newton2[0:1, 0:1])
                        nc.vector.tensor_scalar(r_out[:], r_y[:], mean_var[0:1, 0, 0:1], rstd[0:1, 0:1],
                                                ALU.subtract, ALU.mult).then_inc(row_done, 1)
                        hold(dve, row_stored, (r + 1) * 16, dve_spare)


_INS = ['x', 'adj', 'L0_gnn_W', 'L0_gnn_a']
_OUTS = [((8192, 128), 'float32')]


def kernel(**inputs):
    import numpy as _np
    import concourse.bacc as _bacc
    from concourse import mybir as _mybir
    from concourse.bass_utils import run_bass_kernel_spmd as _run

    nc = _bacc.Bacc("TRN2", target_bir_lowering=False, num_devices=1)
    arrays, args = {}, []
    for name in _INS:
        a = _np.ascontiguousarray(inputs[name])
        arrays[f"in_{name}"] = a
        args.append(nc.dram_tensor(f"in_{name}", a.shape, _mybir.dt.from_np(a.dtype), kind="ExternalInput").ap())
    for i, (shape, dtype) in enumerate(_OUTS):
        dt = _mybir.dt.from_np(_np.dtype(dtype))
        args.append(nc.dram_tensor(f"out_{i}", shape, dt, kind="ExternalOutput").ap())
    graph_attention(nc, *args)
    r = _run(nc, [arrays], core_ids=[0])
    return r.results[0]["out_0"]
```
